# Optimizing a Trainium2 kernel written in Bass

```python
import numpy as np
import jax
import jax.numpy as jnp

def _softmax(x, axis=-1):
    return jax.nn.softmax(x, axis=axis)

def _gelu(x):
    return jax.nn.gelu(x, approximate=True)

def _silu(x):
    return jax.nn.silu(x)

def _sigmoid(x):
    return jax.nn.sigmoid(x)

def _layernorm(x, axis=-1, eps=1e-05):
    m = jnp.mean(x, axis=axis, keepdims=True)
    v = jnp.var(x, axis=axis, keepdims=True)
    return (x - m) / jnp.sqrt(v + eps)

def _scatter_add(tgt, idx, src, axis=0):
    return tgt.at[idx].add(src)

def _segment_sum(src, seg, n):
    return jax.ops.segment_sum(src, seg, n)
kernel_name = 'mk_xattn_ffn_d1_seqx_r2_0ca223'

def setup_inputs(seed: int=0):
    np.random.seed(seed)
    _w = jnp.asarray

    def _rec_inputs():
        import jax
        import jax.numpy as jnp
        _rk = jax.random.key(seed)
        x = 4.136e-05 + 0.9999 * jax.random.normal(jax.random.fold_in(_rk, 1), (4, 1024, 1024), jnp.float32)
        _lenS = 1024 - jax.random.randint(jax.random.fold_in(_rk, 7), (4,), 0, max(1, 1024 // 4) + 1, jnp.int32)
        _lenS2 = 1024 - jax.random.randint(jax.random.fold_in(_rk, 8), (4,), 0, max(1, 1024 // 4) + 1, jnp.int32)
        _ctx_1024P = jax.random.normal(jax.random.fold_in(_rk, 11), (4, 16, 512), jnp.float32)
        _ctx_1024c = jax.random.dirichlet(jax.random.fold_in(_rk, 511), 0.3 * jnp.ones((16,), jnp.float32), (4, 1024))
        _ctx_1024t = jnp.einsum('bsk,bkd->bsd', _ctx_1024c, _ctx_1024P)
        _ctx_1024t = _ctx_1024t * jax.lax.rsqrt(jnp.mean(jnp.square(_ctx_1024t)) + 1e-12) * 0.953939
        ctx_1024 = -0.000292821 + 1.00034 * (_ctx_1024t + 0.3 * jax.random.normal(jax.random.fold_in(_rk, 611), (4, 1024, 512), jnp.float32))
        return (x, ctx_1024)
    x, ctx_1024 = _rec_inputs()

    def _L0_xattn_setup():
        import jax, jax.numpy as jnp
        import numpy as np
        import math
        B, L, DM = (2, 1024, 512)
        DS, DC, EXP = (16, 4, 2)
        DI = EXP * DM
        DR = math.ceil(DM / 16)
        DT_MIN, DT_MAX, DT_FLOOR = (0.001, 0.1, 0.0001)

        def _ssm_forward(hidden_states, z, in_proj_w, conv_w, conv_b, x_proj_w, dt_proj_w, dt_proj_b, A_log, D):
            b = hidden_states.shape[0]
            x = jnp.einsum('ed,bld->bel', in_proj_w, hidden_states)
            xp = jnp.pad(x, ((0, 0), (0, 0), (DC - 1, 0)))
            xc = jax.lax.conv_general_dilated(xp, conv_w[:, None, :], window_strides=(1,), padding='VALID', dimension_numbers=('NCH', 'OIH', 'NCH'), feature_group_count=DI)
            u = jax.nn.silu(xc + conv_b[None, :, None])
            x_dbl = jnp.einsum('ke,bel->bkl', x_proj_w, u)
            dt_lo = x_dbl[:, :DR]
            Bm = x_dbl[:, DR:DR + DS]
            Cm = x_dbl[:, DR + DS:]
            delta = jax.nn.softplus(jnp.einsum('er,brl->bel', dt_proj_w, dt_lo) + dt_proj_b[None, :, None])
            A = -jnp.exp(A_log)

            def step(state, xs):
                d_t, B_t, C_t, u_t = xs
                dA = jnp.exp(d_t[..., None] * A)
                state = state * dA + (d_t * u_t)[..., None] * B_t[:, None, :]
                y_t = jnp.einsum('ben,bn->be', state, C_t)
                return (state, y_t)
            xs = (jnp.moveaxis(delta, -1, 0), jnp.moveaxis(Bm, -1, 0), jnp.moveaxis(Cm, -1, 0), jnp.moveaxis(u, -1, 0))
            state0 = jnp.zeros((b, DI, DS), delta.dtype)
            _, ys = jax.lax.scan(step, state0, xs)
            y = jnp.moveaxis(ys, 0, -1)
            y = y + D[None, :, None] * u
            y = y * jax.nn.silu(z)
            return jnp.swapaxes(y, 1, 2)
        key = jax.random.key(seed)
        ks = jax.random.split(key, 8)
        hidden_states = jax.random.normal(ks[0], (B, L, DM), jnp.float32)
        z = jax.random.normal(ks[1], (B, DI, L), jnp.float32)
        in_proj_w = jax.random.normal(ks[2], (DI, DM), jnp.float32) * DM ** (-0.5)
        conv_w = jax.random.normal(ks[3], (DI, DC), jnp.float32) * DC ** (-0.5)
        conv_b = jnp.zeros((DI,), jnp.float32)
        x_proj_w = jax.random.normal(ks[4], (DR + 2 * DS, DI), jnp.float32) * DI ** (-0.5)
        dt_std = DR ** (-0.5)
        dt_proj_w = jax.random.uniform(ks[5], (DI, DR), jnp.float32, -dt_std, dt_std)
        dt = jnp.exp(jax.random.uniform(ks[6], (DI,), jnp.float32) * (math.log(DT_MAX) - math.log(DT_MIN)) + math.log(DT_MIN))
        dt = jnp.clip(dt, DT_FLOOR)
        dt_proj_b = dt + jnp.log(-jnp.expm1(-dt))
        A_log = jnp.log(jnp.broadcast_to(jnp.arange(1, DS + 1, dtype=jnp.float32), (DI, DS)))
        D = jnp.ones((DI,), jnp.float32)
        return dict(hidden_states=hidden_states, z=z, in_proj_w=in_proj_w, conv_w=conv_w, conv_b=conv_b, x_proj_w=x_proj_w, dt_proj_w=dt_proj_w, dt_proj_b=dt_proj_b, A_log=A_log, D=D)
    _L0_xattn_all = _L0_xattn_setup()
    _L0_xattn_in = {k: v for k, v in _L0_xattn_all.items() if k in ('in_proj_w', 'conv_w', 'conv_b', 'x_proj_w', 'dt_proj_w', 'dt_proj_b', 'A_log', 'D')}
    del _L0_xattn_all

    def _L0_ffn_setup():
        import jax, jax.numpy as jnp
        import numpy as np
        B, S, D_IN, D_OUT = (4, 1024, 1024, 1024)
        E, R, TOP_K = (8, 8, 2)
        ALPHA = 16.0
        SCALE = ALPHA / R
        key = jax.random.key(seed)
        ks = jax.random.split(key, 6)
        x = jax.random.normal(ks[0], (B, S, D_IN), dtype=jnp.float32)
        W_base = jax.random.normal(ks[1], (D_OUT, D_IN), dtype=jnp.float32) / np.sqrt(D_IN)
        b_base = jax.random.normal(ks[2], (D_OUT,), dtype=jnp.float32) * 0.01
        W_router = jax.random.normal(ks[3], (E, D_IN), dtype=jnp.float32) / np.sqrt(D_IN)
        A_w = jax.random.normal(ks[4], (E, R, D_IN), dtype=jnp.float32) / np.sqrt(D_IN)
        B_w = jax.random.normal(ks[5], (E, D_OUT, R), dtype=jnp.float32) * 0.02
        return {'x': x, 'W_base': W_base, 'b_base': b_base, 'W_router': W_router, 'A_w': A_w, 'B_w': B_w}
    _L0_ffn_all = _L0_ffn_setup()
    _L0_ffn_in = {k: v for k, v in _L0_ffn_all.items() if k in ('W_base', 'b_base', 'W_router', 'A_w', 'B_w')}
    del _L0_ffn_all
    return {'x': x, 'ctx_1024': ctx_1024, 'L0_xattn_in_proj_w': _L0_xattn_in['in_proj_w'], 'L0_xattn_conv_w': _L0_xattn_in['conv_w'], 'L0_xattn_conv_b': _L0_xattn_in['conv_b'], 'L0_xattn_x_proj_w': _L0_xattn_in['x_proj_w'], 'L0_xattn_dt_proj_w': _L0_xattn_in['dt_proj_w'], 'L0_xattn_dt_proj_b': _L0_xattn_in['dt_proj_b'], 'L0_xattn_A_log': _L0_xattn_in['A_log'], 'L0_xattn_D': _L0_xattn_in['D'], 'L0_ffn_W_base': _L0_ffn_in['W_base'], 'L0_ffn_b_base': _L0_ffn_in['b_base'], 'L0_ffn_W_router': _L0_ffn_in['W_router'], 'L0_ffn_A_w': _L0_ffn_in['A_w'], 'L0_ffn_B_w': _L0_ffn_in['B_w']}

def reference(x, ctx_1024, L0_xattn_in_proj_w, L0_xattn_conv_w, L0_xattn_conv_b, L0_xattn_x_proj_w, L0_xattn_dt_proj_w, L0_xattn_dt_proj_b, L0_xattn_A_log, L0_xattn_D, L0_ffn_W_base, L0_ffn_b_base, L0_ffn_W_router, L0_ffn_A_w, L0_ffn_B_w):
    import jax
    import jax.numpy as jnp

    def _L0_xattn_ref(hidden_states, z, in_proj_w, conv_w, conv_b, x_proj_w, dt_proj_w, dt_proj_b, A_log, D):
        import jax, jax.numpy as jnp
        import numpy as np
        import math
        B, L, DM = (2, 1024, 512)
        DS, DC, EXP = (16, 4, 2)
        DI = EXP * DM
        DR = math.ceil(DM / 16)
        DT_MIN, DT_MAX, DT_FLOOR = (0.001, 0.1, 0.0001)

        def _ssm_forward(hidden_states, z, in_proj_w, conv_w, conv_b, x_proj_w, dt_proj_w, dt_proj_b, A_log, D):
            b = hidden_states.shape[0]
            x = jnp.einsum('ed,bld->bel', in_proj_w, hidden_states)
            xp = jnp.pad(x, ((0, 0), (0, 0), (DC - 1, 0)))
            xc = jax.lax.conv_general_dilated(xp, conv_w[:, None, :], window_strides=(1,), padding='VALID', dimension_numbers=('NCH', 'OIH', 'NCH'), feature_group_count=DI)
            u = jax.nn.silu(xc + conv_b[None, :, None])
            x_dbl = jnp.einsum('ke,bel->bkl', x_proj_w, u)
            dt_lo = x_dbl[:, :DR]
            Bm = x_dbl[:, DR:DR + DS]
            Cm = x_dbl[:, DR + DS:]
            delta = jax.nn.softplus(jnp.einsum('er,brl->bel', dt_proj_w, dt_lo) + dt_proj_b[None, :, None])
            A = -jnp.exp(A_log)

            def step(state, xs):
                d_t, B_t, C_t, u_t = xs
                dA = jnp.exp(d_t[..., None] * A)
                state = state * dA + (d_t * u_t)[..., None] * B_t[:, None, :]
                y_t = jnp.einsum('ben,bn->be', state, C_t)
                return (state, y_t)
            xs = (jnp.moveaxis(delta, -1, 0), jnp.moveaxis(Bm, -1, 0), jnp.moveaxis(Cm, -1, 0), jnp.moveaxis(u, -1, 0))
            state0 = jnp.zeros((b, DI, DS), delta.dtype)
            _, ys = jax.lax.scan(step, state0, xs)
            y = jnp.moveaxis(ys, 0, -1)
            y = y + D[None, :, None] * u
            y = y * jax.nn.silu(z)
            return jnp.swapaxes(y, 1, 2)
        return _ssm_forward(hidden_states, z, in_proj_w, conv_w, conv_b, x_proj_w, dt_proj_w, dt_proj_b, A_log, D)

    def _L0_ffn_ref(x, W_base, b_base, W_router, A_w, B_w):
        import jax, jax.numpy as jnp
        import numpy as np
        B, S, D_IN, D_OUT = (4, 1024, 1024, 1024)
        E, R, TOP_K = (8, 8, 2)
        ALPHA = 16.0
        SCALE = ALPHA / R
        y = jnp.einsum('bsd,od->bso', x, W_base) + b_base
        logits = jnp.einsum('bsd,ed->bse', x, W_router)
        topk_vals, topk_idx = jax.lax.top_k(logits, TOP_K)
        gates = jax.nn.softmax(topk_vals, axis=-1)
        h = jnp.einsum('bsd,erd->bser', x, A_w)
        expert_outs = jnp.einsum('bser,eor->bseo', h, B_w) * SCALE
        topk_outs = jnp.take_along_axis(expert_outs, topk_idx[..., None], axis=2)
        fused = jnp.sum(topk_outs * gates[..., None], axis=2)
        return y + fused
    x = x + _L0_xattn_ref(ctx_1024, _layernorm(x, axis=-1), L0_xattn_in_proj_w, L0_xattn_conv_w, L0_xattn_conv_b, L0_xattn_x_proj_w, L0_xattn_dt_proj_w, L0_xattn_dt_proj_b, L0_xattn_A_log, L0_xattn_D)
    x = x + _L0_ffn_ref(_layernorm(x, axis=-1), L0_ffn_W_base, L0_ffn_b_base, L0_ffn_W_router, L0_ffn_A_w, L0_ffn_B_w)
    return x

_drawn_inputs = setup_inputs


def setup_inputs(seed=0):
    import zlib

    import numpy as np

    out = dict(_drawn_inputs(seed))
    spreads = {'L0_xattn_conv_b': (0.0, 0.1), 'L0_xattn_D': (1.0, 0.2)}
    factors = {'L0_xattn_dt_proj_w': 4.907, 'L0_ffn_b_base': 8.0}
    for name, (base, spread) in spreads.items():
        noise = np.random.default_rng([zlib.crc32(name.encode()), seed]).standard_normal(out[name].shape)
        drawn = base * np.exp(spread * noise) if base else spread * noise
        out[name] = jnp.asarray(drawn.astype(out[name].dtype))
    for name, factor in factors.items():
        out[name] = (out[name] * factor).astype(out[name].dtype)
    return out
```

```python
import concourse.bass as bass
from concourse import mybir
from contextlib import ExitStack

B, L, DM, DI, DS, DR = 4, 1024, 512, 1024, 16, 32
P = 128
NE = DI // P
NK = DM // P
NC = 4
H = 512
NEX, RANK = 8, 8
NT = B * L // P
SCALE = 16.0 / RANK
EPS = 1e-5
CAP = 40.0
FP32, BF16, U32 = mybir.dt.float32, mybir.dt.bfloat16, mybir.dt.uint32
ALU = mybir.AluOpType
ACT = mybir.ActivationFunctionType


def after(engine, semaphore, count):
    if isinstance(count, int) and count <= 0:
        return
    engine.wait_ge(semaphore, count)


def halves():
    return [slice(h * H, (h + 1) * H) for h in range(L // H)]


def front_stage(nc, x, ctxT, w_inT, w_xT, w_dtT, chan, u_d, delta_d, du_d, sz_d, parts_d):
    with ExitStack() as stack:
        def sb(name, shape, dt=FP32):
            return stack.enter_context(nc.sbuf_tensor(name, shape, dt))

        def sem(name):
            return stack.enter_context(nc.semaphore(name))

        w_in = sb("w_in", [P, NK, DI])
        w_x = sb("w_x", [P, NE, P])
        w_dt = sb("w_dt", [P, DI])
        ch = sb("ch", [P, NE, NC + 2])
        ctx = sb("ctx", [P, NK, L])
        xr = sb("xr", [P, NE, L])
        u = sb("u", [P, NE, L])
        conv = sb("conv", [P, 2, L])
        xd = sb("xd", [P, L])
        rest = sb("rest", [96, L])
        parts = sb("parts", [96, L], BF16)
        mid = sb("mid", [96, L], BF16)
        v = sb("v", [P, 2, L])
        ex = sb("ex", [P, 2, L])
        ex1 = sb("ex1", [P, 2, L])
        ln = sb("ln", [P, 2, L])
        delta = sb("delta", [P, 2, L])
        du = sb("du", [P, 2, L])
        stats = sb("stats", [P, NE, 2, 6])
        mv = sb("mv", [P, NE, 2])
        std = sb("std", [P, NE])
        rstd = sb("rstd", [P, NE])
        nbias = sb("nbias", [P, NE])
        eps = sb("eps1", [P, 1])
        pause = sb("pause1", [P, 2])
        x_ps = [stack.enter_context(nc.psum_tensor(f"x_ps{i}", [P, L], FP32)) for i in range(2)]
        xd_ps = stack.enter_context(nc.psum_tensor("xd_ps", [P, L], FP32))
        v_ps = stack.enter_context(nc.psum_tensor("v_ps", [P, L], FP32))

        weights_in, ctx_in, xr_in = sem("weights_in"), sem("ctx_in"), sem("xr_in")
        x_ready, conv_begun, conv_step, conv_done = sem("x_ready"), sem("conv_begun"), sem("conv_step"), sem("conv_done")
        u_ready, xd_ready, xd_copied = sem("u_ready"), sem("xd_ready"), sem("xd_copied")
        split_step, split_done = sem("split_step"), sem("split_done")
        v_ready, v_copied, arg_ready, ex_ready = sem("v_ready"), sem("v_copied"), sem("arg_ready"), sem("ex_ready")
        ex1_ready, ln_ready, err_ready, sum_ready = sem("ex1_ready"), sem("ln_ready"), sem("err_ready"), sem("sum_ready")
        delta_ready, du_ready = sem("delta_ready"), sem("du_ready")
        eps_set, stats_ready, mv_ready, std_ready, rstd_ready, nbias_ready, sz_ready = (
            sem(n) for n in ("eps_set", "stats_ready", "mv_ready", "std_ready", "rstd_ready", "nbias_ready", "sz_ready"))
        u_out, parts_out, sz_out = sem("u_out"), sem("parts_out"), sem("sz_out")
        delta_out = [sem(f"delta_out{i}") for i in range(2)]
        du_out = [sem(f"du_out{i}") for i in range(2)]

        def batches(engine, body):
            body(0)
            with engine.Fori(1, B) as b:
                body(b)

        block = stack.enter_context(nc.Block())

        @block.sync
        def _(sp):
            sp.dma_start(w_in[:, :, :], w_inT.rearrange("(k p) e -> p k e", p=P)).then_inc(weights_in, 16)
            sp.dma_start(w_x[:, :, :], w_xT.rearrange("(k p) e -> p k e", p=P)).then_inc(weights_in, 16)
            sp.dma_start(w_dt[96:96 + DR, :], w_dtT).then_inc(weights_in, 16)
            sp.dma_start(ch[:, :, :], chan.rearrange("(k p) c -> p k c", p=P)).then_inc(weights_in, 16)

            def body(b):
                after(sp, x_ready, b * NE)
                sp.dma_start(ctx[:, :, :], ctxT[bass.ds(b, 1)].rearrange("o (k p) l -> p (o k) l", p=P)).then_inc(ctx_in, 16)
                after(sp, sz_out, b * 16)
                sp.dma_start(xr[:, :, :], x[bass.ds(b, 1)].rearrange("o (k p) l -> p (o k) l", p=P)).then_inc(xr_in, 16)
                sp.wait_ge(sz_ready, b * NE + NE)
                sp.dma_start(sz_d[bass.ds(b, 1)].rearrange("o (k p) l -> p (o k) l", p=P), xr[:, :, :]).then_inc(sz_out, 16)
                sp.wait_ge(u_ready, b * NE + NE)
                sp.dma_start(u_d[bass.ds(b, 1)].rearrange("o (k p) l -> p (o k) l", p=P), u[:, :, :]).then_inc(u_out, 16)
                sp.wait_ge(split_done, b + 1)
                sp.dma_start(parts_d[bass.ds(b, 1)].rearrange("o p l -> (o p) l"), parts[:, :]).then_inc(parts_out, 16)
                for t in range(NE):
                    sp.wait_ge(delta_ready, b * NE + t + 1)
                    sp.dma_start(delta_d[bass.ds(b, 1), t * P:(t + 1) * P].rearrange("o p l -> (o p) l"), delta[:, t % 2, :]).then_inc(delta_out[t % 2], 16)
                    sp.wait_ge(du_ready, b * NE + t + 1)
                    sp.dma_start(du_d[bass.ds(b, 1), t * P:(t + 1) * P].rearrange("o p l -> (o p) l"), du[:, t % 2, :]).then_inc(du_out[t % 2], 16)
            batches(sp, body)
            sp.wait_ge(sz_out, 16 * B)
            sp.wait_ge(u_out, 16 * B)
            sp.wait_ge(parts_out, 16 * B)
            for i in range(2):
                sp.wait_ge(delta_out[i], 16 * B * NE // 2)
                sp.wait_ge(du_out[i], 16 * B * NE // 2)

        @block.tensor
        def _(pe):
            pe.wait_ge(weights_in, 64)

            def body(b):
                def project(t):
                    if t == 0:
                        pe.wait_ge(ctx_in, b * 16 + 16)
                    after(pe, conv_done, b * NE + t - 1)
                    for hs in halves():
                        for k in range(NK):
                            last = nc.tensor.matmul(x_ps[t % 2][:, hs], w_in[:, k, t * P:(t + 1) * P], ctx[:, k, hs],
                                                    start=(k == 0), stop=(k == NK - 1))
                    last.then_inc(x_ready, 1)

                project(0)
                for t in range(NE):
                    if t + 1 < NE:
                        project(t + 1)
                    if t == 0:
                        after(pe, xd_copied, b)
                    pe.wait_ge(u_ready, b * NE + t + 1)
                    for hs in halves():
                        last = nc.tensor.matmul(xd_ps[:, hs], w_x[:, t, :], u[:, t, hs], start=(t == 0), stop=(t == NE - 1))
                last.then_inc(xd_ready, 1)
                pe.wait_ge(xd_copied, b + 1)
                for t in range(NE):
                    after(pe, v_copied, b * NE + t)
                    for hs in halves():
                        last = nc.tensor.matmul(v_ps[:, hs], w_dt[96:96 + DR, t * P:(t + 1) * P], xd[96:96 + DR, hs], start=True, stop=True)
                    last.then_inc(v_ready, 1)
            batches(pe, body)

        @block.scalar
        def _(act):
            act.wait_ge(weights_in, 64)

            def body(b):
                act.wait_ge(mv_ready, b * NE + NE)
                if isinstance(b, int):
                    act.wait_ge(eps_set, 1)
                nc.scalar.activation(std[:, :], mv[:, :, 1], ACT.Sqrt, bias=eps[:, :]).then_inc(std_ready, 1)
                for t in range(NE):
                    act.wait_ge(x_ready, b * NE + t + 1)
                    after(act, u_ready, b * NE + t - 1)
                    nc.scalar.activation(conv[:, t % 2, :], x_ps[t % 2][:, :], ACT.Identity, bias=ch[:, t, NC:NC + 1],
                                         scale=ch[:, t, NC - 1:NC]).then_inc(conv_begun, 1)
                    if t == 0:
                        act.wait_ge(nbias_ready, b + 1)
                    nc.scalar.activation(xr[:, t, :], xr[:, t, :], ACT.Silu, bias=nbias[:, t:t + 1],
                                         scale=rstd[:, t:t + 1]).then_inc(sz_ready, 1)
                    if t == 0:
                        after(act, u_out, b * 16)
                        after(act, du_ready, b * NE)
                    act.wait_ge(conv_done, b * NE + t + 1)
                    nc.scalar.activation(u[:, t, :], conv[:, t % 2, :], ACT.Silu).then_inc(u_ready, 1)
                act.wait_ge(xd_ready, b + 1)
                after(act, v_ready, b * NE)
                after(act, split_done, b)
                nc.scalar.activation(xd[:, :], xd_ps[:, :], ACT.Copy).then_inc(xd_copied, 1)
                for t in range(NE + 1):
                    if t < NE:
                        act.wait_ge(arg_ready, b * NE + t + 1)
                        nc.scalar.activation(ex[:, t % 2, :], ex[:, t % 2, :], ACT.Exp).then_inc(ex_ready, 1)
                    if t > 0:
                        act.wait_ge(ex1_ready, b * NE + t)
                        after(act, sum_ready, b * NE + t - 2)
                        nc.scalar.activation(ln[:, (t - 1) % 2, :], ex1[:, (t - 1) % 2, :], ACT.Ln).then_inc(ln_ready, 1)
            batches(act, body)

        @block.vector
        def _(dve):
            nc.vector.memset(eps[:, :], EPS).then_inc(eps_set, 1)
            dve.wait_ge(weights_in, 64)

            def body(b):
                dve.wait_ge(xr_in, b * 16 + 16)
                for t in range(NE):
                    for i, hs in enumerate(halves()):
                        nc.vector.bn_stats(stats[:, t, i, :], xr[:, t, hs]).then_inc(stats_ready, 1)
                after(dve, std_ready, b)
                nc.vector.memset(pause[:, 0:1], 0.0)
                dve.wait_ge(stats_ready, b * 2 * NE + 2 * NE)
                nc.vector.memset(pause[:, 1:2], 0.0)
                for t in range(NE):
                    nc.vector.bn_aggr(mv[:, t, :], stats[:, t, :, :]).then_inc(mv_ready, 1)
                dve.wait_ge(std_ready, b + 1)
                nc.vector.reciprocal(rstd[:, :], std[:, :]).then_inc(rstd_ready, 1)
                dve.wait_ge(rstd_ready, b + 1)
                nc.vector.scalar_tensor_tensor(nbias[:, :], mv[:, :, 0], -1.0, rstd[:, :], ALU.mult, ALU.mult).then_inc(nbias_ready, 1)
                for t in range(NE):
                    dve.wait_ge(conv_begun, b * NE + t + 1)
                    for back in range(1, NC):
                        if back > 1:
                            dve.wait_ge(conv_step, (b * NE + t) * (NC - 2) + back - 1)
                        nc.vector.scalar_tensor_tensor(
                            conv[:, t % 2, back:], x_ps[t % 2][:, 0:L - back], ch[:, t, NC - 1 - back:NC - back],
                            conv[:, t % 2, back:], ALU.mult, ALU.add).then_inc(conv_step if back < NC - 1 else conv_done, 1)
                dve.wait_ge(xd_copied, b + 1)
                after(dve, parts_out, b * 16)
                split = [
                    lambda: nc.vector.tensor_copy(parts[:, :], xd[0:96, :]),
                    lambda: nc.vector.tensor_tensor(rest[:, :], xd[0:96, :], parts[:, :], ALU.subtract),
                    lambda: nc.vector.tensor_copy(mid[:, :], rest[:, :]),
                    lambda: nc.vector.tensor_tensor(rest[:, :], rest[:, :], mid[:, :], ALU.subtract),
                    lambda: nc.vector.tensor_copy(parts[32:64, :], mid[32:64, :]),
                ]
                for i, step in enumerate(split):
                    step().then_inc(split_step, 1)
                    dve.wait_ge(split_step, b * len(split) + i + 1)
                nc.vector.tensor_copy(parts[64:96, :], rest[64:96, :]).then_inc(split_done, 1)

                def take(t):
                    dve.wait_ge(v_ready, b * NE + t + 1)
                    after(dve, delta_ready, b * NE + t - 1)
                    nc.vector.tensor_scalar(v[:, t % 2, :], v_ps[:, :], ch[:, t, NC + 1:NC + 2], None, ALU.add).then_inc(v_copied, 1)
                    dve.wait_ge(v_copied, b * NE + t + 1)
                    after(dve, sum_ready, b * NE + t - 1)
                    nc.vector.tensor_scalar(ex[:, t % 2, :], v[:, t % 2, :], CAP, None, ALU.min).then_inc(arg_ready, 1)

                def one_plus(t):
                    dve.wait_ge(ex_ready, b * NE + t + 1)
                    after(dve, ln_ready, b * NE + t - 1)
                    nc.vector.tensor_scalar(ex1[:, t % 2, :], ex[:, t % 2, :], 1.0, None, ALU.add).then_inc(ex1_ready, 1)
                    dve.wait_ge(ex1_ready, b * NE + t + 1)
                    nc.vector.scalar_tensor_tensor(ex[:, t % 2, :], ex1[:, t % 2, :], -1.0, ex[:, t % 2, :], ALU.add, ALU.subtract).then_inc(err_ready, 1)

                def finish(t):
                    dve.wait_ge(sum_ready, b * NE + t + 1)
                    after(dve, delta_out[t % 2], b * (NE * 8) + t // 2 * 16)
                    after(dve, du_ready, b * NE + t - 1)
                    nc.vector.tensor_tensor(delta[:, t % 2, :], ln[:, t % 2, :], v[:, t % 2, :], ALU.max).then_inc(delta_ready, 1)

                for t in range(NE + 2):
                    if t >= 2:
                        finish(t - 2)
                    if t < NE:
                        take(t)
                    if 1 <= t <= NE:
                        one_plus(t - 1)
            batches(dve, body)

        @block.gpsimd
        def _(pool):
            def body(b):
                for t in range(NE + 1):
                    if t < NE:
                        pool.wait_ge(ln_ready, b * NE + t + 1)
                        pool.wait_ge(err_ready, b * NE + t + 1)
                        nc.gpsimd.tensor_tensor(ln[:, t % 2, :], ln[:, t % 2, :], ex[:, t % 2, :], ALU.subtract).then_inc(sum_ready, 1)
                    if t > 0:
                        pool.wait_ge(delta_ready, b * NE + t)
                        after(pool, du_out[(t - 1) % 2], b * (NE * 8) + (t - 1) // 2 * 16)
                        nc.gpsimd.tensor_tensor(du[:, (t - 1) % 2, :], delta[:, (t - 1) % 2, :], u[:, t - 1, :], ALU.mult).then_inc(du_ready, 1)
            batches(pool, body)


def scan_stage(nc, chan2, a_log, pick, ident_d, u_d, delta_d, du_d, sz_d, parts_d, yy_d):
    NB = 4
    LAG = 2
    with ExitStack() as stack:
        def sb(name, shape, dt=FP32):
            return stack.enter_context(nc.sbuf_tensor(name, shape, dt))

        def sem(name):
            return stack.enter_context(nc.semaphore(name))

        a = sb("a", [P, NE, DS])
        d_ch = sb("d_ch", [P, NE])
        sel = sb("sel", [96, 2 * DS, P], BF16)
        ident = sb("ident", [P, P])
        parts = sb("parts2", [96, L], BF16)
        c_all = sb("c_all", [P, DS, L])
        delta = sb("delta2", [P, 2, L])
        du = sb("du2", [P, 2, L])
        u = sb("u2", [P, 2, L])
        sz = sb("sz2", [P, 2, L])
        dbu = sb("dbu", [P, 2, L])
        state = sb("state", [P, NB, L])
        prod = sb("prod", [P, NB, L])
        y = sb("y", [P, L])
        gated = sb("gated", [P, L])
        yy = sb("yy", [P, 2, L])
        decay = [stack.enter_context(nc.psum_tensor(f"decay{i}", [P, L], FP32)) for i in range(2)]
        row = stack.enter_context(nc.psum_tensor("row", [P, L], FP32))
        y_ps = stack.enter_context(nc.psum_tensor("y_ps", [P, L], FP32))

        consts_in, a_step, parts_in = sem("consts_in"), sem("a_step"), sem("parts_in")
        tiles_in = [sem(f"tiles_in{i}") for i in range(2)]
        late_in = [sem(f"late_in{i}") for i in range(2)]
        c_ready, c_copied, b_ready = sem("c_ready"), sem("c_copied"), sem("b_ready")
        decay_ready, dbu_ready, scan_done = sem("decay_ready"), sem("dbu_ready"), sem("scan_done")
        prod_ready, summed, y_copied = sem("prod_ready"), sem("summed"), sem("y_copied")
        skip_added, yy_ready = sem("skip_added"), sem("yy_ready")
        yy_out = [sem(f"yy_out{i}") for i in range(2)]

        def blocks(engine, body):
            body(0, 0, 0, 0, True)
            body(1, 1, 1, 0, False)
            body(2, 0, 2, 0, False)
            with engine.Fori(0, B - 1) as b:
                with engine.Fori(0, (NE - 4) // 2) as q:
                    for s in (3, 4):
                        body(b * NE + q * 2 + s, s % 2, q * 2 + s, b, False)
                body(b * NE + NE - 1, 1, NE - 1, b, False)
                body(b * NE + NE, 0, 0, b + 1, True)
                body(b * NE + NE + 1, 1, 1, b + 1, False)
                body(b * NE + NE + 2, 0, 2, b + 1, False)
            with engine.Fori(0, (NE - 4) // 2) as q:
                for s in (3, 4):
                    body(q * 2 + ((B - 1) * NE + s), s % 2, q * 2 + s, B - 1, False)
            body(B * NE - 1, 1, NE - 1, B - 1, False)

        def rows_of(dram, E):
            return dram.rearrange("b (k p) l -> (b k) p l", p=P)[bass.ds(E, 1)].rearrange("o p l -> (o p) l")

        block = stack.enter_context(nc.Block())

        @block.sync
        def _(sp):
            sp.dma_start(a[:, :, :], a_log.rearrange("(k p) n -> p k n", p=P)).then_inc(consts_in, 16)
            sp.dma_start(d_ch[:, :], chan2).then_inc(consts_in, 16)
            sp.dma_start(sel[:, :, :], pick).then_inc(consts_in, 16)
            sp.dma_start(ident[:, :], ident_d).then_inc(consts_in, 16)

            def load(E, slot, t, b, fills):
                if fills:
                    after(sp, b_ready, b * NE * DS)
                    sp.dma_start(parts[:, :], parts_d[bass.ds(b, 1)].rearrange("o p l -> (o p) l")).then_inc(parts_in, 16)
                after(sp, decay_ready, E * DS - DS)
                after(sp, dbu_ready, E * DS - DS)
                sp.dma_start(delta[:, slot, :], rows_of(delta_d, E)).then_inc(tiles_in[slot], 16)
                sp.dma_start(du[:, slot, :], rows_of(du_d, E)).then_inc(tiles_in[slot], 16)
                after(sp, yy_ready, E - 1)
                sp.dma_start(u[:, slot, :], rows_of(u_d, E)).then_inc(late_in[slot], 16)
                sp.dma_start(sz[:, slot, :], rows_of(sz_d, E)).then_inc(late_in[slot], 16)
            blocks(sp, load)

        @block.tensor
        def _(pe):
            pe.wait_ge(consts_in, 64)

            def spread(n):
                for hs in halves():
                    last = nc.tensor.matmul(row[:, hs], sel[:, n, :], parts[:, hs], start=True, stop=True)
                return last

            def add_up(E, n):
                pe.wait_ge(prod_ready, E * DS + n + 1)
                if n == 0:
                    after(pe, y_copied, E)
                for hs in halves():
                    last = nc.tensor.matmul(y_ps[:, hs], ident[:, :], prod[:, n % NB, hs], start=(n == 0), stop=(n == DS - 1))
                last.then_inc(summed, 1)

            def body(E, slot, t, b, fills):
                if fills:
                    pe.wait_ge(parts_in, b * 16 + 16)
                for n in range(DS):
                    U = E * DS + n
                    after(pe, dbu_ready, U)
                    if fills:
                        spread(DS + n).then_inc(c_ready, 1)
                        pe.wait_ge(c_copied, b * DS + n + 1)
                    spread(n).then_inc(b_ready, 1)
                    if n >= LAG:
                        add_up(E, n - LAG)
                    elif not (isinstance(E, int) and E == 0):
                        add_up(E - 1, n - LAG + DS)
            blocks(pe, body)
            for n in range(DS - LAG, DS):
                add_up(B * NE - 1, n)

        @block.scalar
        def _(act):
            act.wait_ge(consts_in, 64)
            nc.scalar.activation(a[:, :, :], a[:, :, :], ACT.Exp).then_inc(a_step, 1)
            act.wait_ge(a_step, 1)
            nc.scalar.activation(a[:, :, :], a[:, :, :], ACT.Copy, scale=-1.0).then_inc(a_step, 1)
            act.wait_ge(a_step, 2)

            def copy_y(E):
                act.wait_ge(summed, E * DS + DS)
                after(act, skip_added, E)
                nc.scalar.activation(y[:, :], y_ps[:, :], ACT.Copy).then_inc(y_copied, 1)

            def body(E, slot, t, b, fills):
                act.wait_ge(tiles_in[slot], (E - slot) * 16 + 32)
                for n in range(DS):
                    U = E * DS + n
                    if n == 3 and not (isinstance(E, int) and E == 0):
                        copy_y(E - 1)
                    after(act, scan_done, U - 1)
                    scale = a[:, t, n:n + 1] if isinstance(t, int) else a[:, bass.ds(t, 1), n:n + 1].rearrange("p o n -> p (o n)")
                    nc.scalar.activation(decay[n % 2][:, :], delta[:, slot, :], ACT.Exp, scale=scale).then_inc(decay_ready, 1)
                    if fills:
                        act.wait_ge(c_ready, b * DS + n + 1)
                        after(act, prod_ready, E * DS - DS + n + 1)
                        nc.scalar.activation(c_all[:, n, :], row[:, :], ACT.Copy).then_inc(c_copied, 1)
            blocks(act, body)
            copy_y(B * NE - 1)

        @block.vector
        def _(dve):
            dve.wait_ge(consts_in, 64)

            def gate(E, slot, t):
                dve.wait_ge(y_copied, E + 1)
                dve.wait_ge(late_in[slot], (E - slot) * 16 + 32)
                scalar = d_ch[:, t:t + 1] if isinstance(t, int) else d_ch[:, bass.ds(t, 1)]
                nc.vector.scalar_tensor_tensor(gated[:, :], u[:, slot, :], scalar, y[:, :], ALU.mult, ALU.add).then_inc(skip_added, 1)
                dve.wait_ge(skip_added, E + 1)
                after(dve, yy_out[slot], (E - slot) * 8)
                nc.vector.tensor_tensor(yy[:, slot, :], gated[:, :], sz[:, slot, :], ALU.mult).then_inc(yy_ready, 1)

            def body(E, slot, t, b, fills):
                dve.wait_ge(tiles_in[slot], (E - slot) * 16 + 32)

                def drive(n):
                    dve.wait_ge(b_ready, E * DS + n + 1)
                    after(dve, scan_done, E * DS + n - 1)
                    nc.vector.tensor_tensor(dbu[:, n % 2, :], du[:, slot, :], row[:, :], ALU.mult).then_inc(dbu_ready, 1)

                drive(0)
                for n in range(DS):
                    if n + 1 < DS:
                        drive(n + 1)
                    U = E * DS + n
                    dve.wait_ge(dbu_ready, U + 1)
                    dve.wait_ge(decay_ready, U + 1)
                    after(dve, prod_ready, U + 1 - NB)
                    nc.vector.tensor_tensor_scan(state[:, n % NB, :], decay[n % 2][:, :], dbu[:, n % 2, :], 0.0,
                                                 ALU.mult, ALU.add).then_inc(scan_done, 1)
                    if n == 7 and not (isinstance(E, int) and E == 0):
                        gate(E - 1, 1 - slot, (NE - 1) if fills else t - 1)
            blocks(dve, body)
            gate(B * NE - 1, 1, NE - 1)

        @block.gpsimd
        def _(pool):
            def store(E, slot):
                pool.wait_ge(yy_ready, E + 1)
                pool.dma_start(rows_of(yy_d, E), yy[:, slot, :]).then_inc(yy_out[slot], 16)

            def body(E, slot, t, b, fills):
                for n in range(DS):
                    U = E * DS + n
                    pool.wait_ge(scan_done, U + 1)
                    if fills:
                        pool.wait_ge(c_copied, b * DS + n + 1)
                    after(pool, summed, U + 1 - NB)
                    nc.gpsimd.tensor_tensor(prod[:, n % NB, :], state[:, n % NB, :], c_all[:, n, :], ALU.mult).then_inc(prod_ready, 1)
                    if n == 12 and not (isinstance(E, int) and E == 0):
                        store(E - 1, 1 - slot)
            blocks(pool, body)
            store(B * NE - 1, 1)
            for i in range(2):
                pool.wait_ge(yy_out[i], 16 * B * NE // 2)


def dense_stage(nc, x, yy_d, w_oT, w_raT, w_bT, ident_d, iota_d, out):
    with ExitStack() as stack:
        def sb(name, shape, dt=FP32):
            return stack.enter_context(nc.sbuf_tensor(name, shape, dt))

        def sem(name):
            return stack.enter_context(nc.semaphore(name))

        NH = NEX * RANK
        w_o = sb("w_o", [P, NE, DI])
        w_ra = sb("w_ra", [P, NE, NH + NEX])
        w_b = sb("w_b", [NH + 1, DI])
        ident = sb("ident3", [P, P])
        iota = sb("iota", [P, NEX])
        yyt = sb("yyt", [P, 2, NE, P])
        xt = sb("xt", [P, 2, DI])
        x1 = sb("x1", [P, 2, DI])
        xn = sb("xn", [P, DI])
        xnT = sb("xnT", [P, 2, NE, P])
        res = sb("res", [P, 2, DI])
        stats = sb("stats3", [P, 2, 6])
        mv = sb("mv3", [P, 2])
        std = sb("std3", [P, 1])
        rstd = sb("rstd3", [P, 1])
        eps = sb("eps3", [P, 1])
        pause = sb("pause3", [P, 2])
        logit = sb("logit", [P, NEX])
        top = sb("top", [P, 8])
        topi = sb("topi", [P, 8], U32)
        topf = sb("topf", [P, 8])
        gap = sb("gap", [P, 1])
        egap = sb("egap", [P, 1])
        esum = sb("esum", [P, 1])
        gate1 = sb("gate1", [P, 1])
        gate2 = sb("gate2", [P, 1])
        mask = sb("mask", [P, 2, NEX])
        gm = sb("gm", [P, NEX])
        g = sb("g", [P, NH + 1])
        gT = sb("gT", [NH + 1, P])
        turn = [stack.enter_context(nc.psum_tensor(f"turn{i}", [P, DI], FP32)) for i in range(1)][0]
        o_ps = [stack.enter_context(nc.psum_tensor(f"o_ps{i}", [P, DI], FP32)) for i in range(2)]
        ra_ps = stack.enter_context(nc.psum_tensor("ra_ps", [P, H], FP32))
        gT_ps = stack.enter_context(nc.psum_tensor("gT_ps", [P, H], FP32))

        consts_in, ones_set = sem("consts_in3"), sem("ones_set")
        tile_in = [sem(f"tile_in{i}") for i in range(2)]
        yy_turned, x1_ready, stats_ready, mv_ready, std_ready, rstd_ready, xn_ready = (
            sem(n) for n in ("yy_turned", "x1_ready", "stats3_ready", "mv3_ready", "std3_ready", "rstd3_ready", "xn_ready"))
        xn_turned, xnT_ready, ra_ready, h_step, gap_ready, egap_ready, g_ready = (
            sem(n) for n in ("xn_turned", "xnT_ready", "ra_ready", "h_step", "gap_ready", "egap_ready", "g_ready"))
        g_turned, gT_ready, o_ready, res_ready = (sem(n) for n in ("g_turned", "gT_ready", "o_ready", "res_ready"))
        res_out = [sem(f"res_out{i}") for i in range(2)]
        STEPS = 10

        xr = x.rearrange("b (k p) l -> (b k) p l", p=P)
        outr = out.rearrange("b (k p) l -> (b k) p l", p=P)
        yyr = yy_d.rearrange("b (k p) (j c) -> b j p k c", p=P, c=P)

        def tiles(engine, body, ahead):
            body(0, 0, 0, 0)
            body(1, 0, 1, 1)
            with engine.Fori(1, NT // 2 - 1) as q:
                body(q * 2, None, None, 0)
                body(q * 2 + 1, None, None, 1)
            body(NT - 2, None, None, 0)
            body(NT - 1, None, None, 1)

        block = stack.enter_context(nc.Block())

        @block.sync
        def _(sp):
            sp.dma_start(ident[:, :], ident_d).then_inc(consts_in, 16)
            sp.dma_start(w_ra[:, :, :], w_raT.rearrange("(k p) n -> p k n", p=P)).then_inc(consts_in, 16)
            sp.dma_start(w_b[:, :], w_bT).then_inc(consts_in, 16)
            sp.dma_start(iota[:, :], iota_d).then_inc(consts_in, 16)
            sp.dma_start(w_o[:, :, :], w_oT.rearrange("(k p) n -> p k n", p=P)).then_inc(consts_in, 16)

            def load(j, slot, b, i):
                after(sp, x1_ready, j - 1)
                sp.dma_start(yyt[:, slot, :, :], yyr[bass.ds(b, 1), bass.ds(i, 1)].rearrange("o r p k c -> (o r p) k c")).then_inc(tile_in[slot], 16)
                sp.dma_start(xt[:, slot, :], xr[bass.ds(j, 1)].rearrange("o p l -> (o p) l")).then_inc(tile_in[slot], 16)
            for i in range(2):
                load(i, i, 0, i)
            with sp.Fori(1, NE // 2) as i:
                for s in range(2):
                    load(i * 2 + s, s, 0, i * 2 + s)
            with sp.Fori(1, B) as b:
                with sp.Fori(0, NE // 2) as i:
                    for s in range(2):
                        load(b * NE + i * 2 + s, s, b, i * 2 + s)

        @block.gpsimd
        def _(pool):
            def body(j, b, i, slot):
                pool.wait_ge(res_ready, j + 1)
                pool.dma_start(outr[bass.ds(j, 1)].rearrange("o p l -> (o p) l"), res[:, slot, :]).then_inc(res_out[slot], 16)
            tiles(pool, body, False)
            for i in range(2):
                pool.wait_ge(res_out[i], 16 * NT // 2)

        @block.tensor
        def _(pe):
            pe.wait_ge(consts_in, 80)

            def turn_yy(j, slot):
                pe.wait_ge(tile_in[slot], (j - slot) * 16 + 32)
                after(pe, xnT_ready, j)
                for k in range(NE):
                    last = nc.tensor.transpose(turn[:, k * P:(k + 1) * P], yyt[:, slot, k, :], ident[:, :])
                last.then_inc(yy_turned, 1)

            def turn_xn(j):
                pe.wait_ge(xn_ready, j + 1)
                for k in range(NE):
                    last = nc.tensor.transpose(turn[:, k * P:(k + 1) * P], xn[:, k * P:(k + 1) * P], ident[:, :])
                last.then_inc(xn_turned, 1)

            def route(j, slot):
                pe.wait_ge(xnT_ready, j + 1)
                after(pe, g_ready, j)
                for k in range(NE):
                    last = nc.tensor.matmul(ra_ps[:, 0:NH + NEX], xnT[:, slot, k, :], w_ra[:, k, :], start=(k == 0), stop=(k == NE - 1))
                last.then_inc(ra_ready, 1)

            def dense(slot, hs):
                for k in range(NE):
                    nc.tensor.matmul(o_ps[slot][:, hs], xnT[:, slot, k, :], w_o[:, k, hs], start=(k == 0), stop=False)

            def body(j, b, i, slot, more=True):
                if more:
                    turn_yy(j + 1, 1 - slot)
                after(pe, res_ready, j - 1)
                dense(slot, halves()[0])
                pe.wait_ge(g_ready, j + 1)
                after(pe, gT_ready, j)
                nc.tensor.transpose(gT_ps[0:NH + 1, 0:P], g[:, :], ident[:, :]).then_inc(g_turned, 1)
                if more:
                    turn_xn(j + 1)
                dense(slot, halves()[1])
                pe.wait_ge(gT_ready, j + 1)
                for hs in halves():
                    last = nc.tensor.matmul(o_ps[slot][:, hs], gT[:, :], w_b[:, hs], start=False, stop=True)
                last.then_inc(o_ready, 1)
                if more:
                    route(j + 1, 1 - slot)

            turn_yy(0, 0)
            turn_xn(0)
            route(0, 0)
            body(0, 0, 0, 0)
            body(1, 0, 0, 1)
            with pe.Fori(1, NT // 2 - 1) as q:
                body(q * 2, 0, 0, 0)
                body(q * 2 + 1, 0, 0, 1)
            body(NT - 2, 0, 0, 0)
            body(NT - 1, 0, 0, 1, more=False)

        @block.scalar
        def _(act):
            def body(j, b, i, slot):
                act.wait_ge(mv_ready, j + 1)
                nc.scalar.activation(std[:, :], mv[:, 1:2], ACT.Sqrt, bias=eps[:, :]).then_inc(std_ready, 1)
                act.wait_ge(xn_turned, j + 1)
                after(act, o_ready, j - 1)
                nc.scalar.activation(xnT[:, slot, :, :], turn[:, :], ACT.Copy).then_inc(xnT_ready, 1)
                act.wait_ge(gap_ready, j + 1)
                nc.scalar.activation(egap[:, :], gap[:, :], ACT.Exp).then_inc(egap_ready, 1)
                act.wait_ge(g_turned, j + 1)
                after(act, o_ready, j)
                nc.scalar.activation(gT[:, :], gT_ps[0:NH + 1, 0:P], ACT.Copy).then_inc(gT_ready, 1)
            tiles(act, body, False)

        @block.vector
        def _(dve):
            nc.vector.memset(eps[:, :], EPS)
            nc.vector.memset(g[:, NH:NH + 1], 1.0).then_inc(ones_set, 1)
            dve.wait_ge(ones_set, 1)
            dve.wait_ge(consts_in, 80)

            def normalise(j, slot):
                dve.wait_ge(yy_turned, j + 1)
                after(dve, res_ready, j - 1)
                nc.vector.tensor_tensor(x1[:, slot, :], xt[:, slot, :], turn[:, :], ALU.add).then_inc(x1_ready, 1)
                dve.wait_ge(x1_ready, j + 1)
                for i, hs in enumerate(halves()):
                    nc.vector.bn_stats(stats[:, i, :], x1[:, slot, hs]).then_inc(stats_ready, 1)
                dve.wait_ge(stats_ready, j * 2 + 2)
                nc.vector.memset(pause[:, 0:1], 0.0)
                nc.vector.bn_aggr(mv[:, :], stats[:, :, :]).then_inc(mv_ready, 1)
                dve.wait_ge(std_ready, j + 1)
                nc.vector.reciprocal(rstd[:, :], std[:, :]).then_inc(rstd_ready, 1)
                dve.wait_ge(rstd_ready, j + 1)
                after(dve, xn_turned, j)
                nc.vector.tensor_scalar(xn[:, :], x1[:, slot, :], mv[:, 0:1], rstd[:, :], ALU.subtract, ALU.mult).then_inc(xn_ready, 1)

            def choose(j):
                links = [0]

                def link(instruction):
                    links[0] += 1
                    instruction.then_inc(h_step, 1)
                    dve.wait_ge(h_step, j * STEPS + links[0])

                dve.wait_ge(ra_ready, j + 1)
                link(nc.vector.tensor_copy(logit[:, :], ra_ps[:, NH:NH + NEX]))
                nc.vector.memset(pause[:, 1:2], 0.0)
                link(nc.vector.max(top[:, :], logit[:, :]))
                nc.vector.tensor_tensor(gap[:, :], top[:, 1:2], top[:, 0:1], ALU.subtract).then_inc(gap_ready, 1)
                link(nc.vector.max_index(topi[:, :], top[:, :], logit[:, :]))
                link(nc.vector.tensor_copy(topf[:, :], topi[:, :]))
                dve.wait_ge(egap_ready, j + 1)
                link(nc.vector.tensor_scalar(esum[:, :], egap[:, :], 1.0, 1.0 / SCALE, ALU.add, ALU.mult))
                link(nc.vector.reciprocal(gate1[:, :], esum[:, :]))
                link(nc.vector.tensor_tensor(gate2[:, :], gate1[:, :], egap[:, :], ALU.mult))
                link(nc.vector.tensor_scalar(mask[:, 0, :], iota[:, :], topf[:, 0:1], gate1[:, :], ALU.is_equal, ALU.mult))
                link(nc.vector.tensor_scalar(mask[:, 1, :], iota[:, :], topf[:, 1:2], gate2[:, :], ALU.is_equal, ALU.mult))
                link(nc.vector.tensor_tensor(gm[:, :], mask[:, 0, :], mask[:, 1, :], ALU.add))
                assert links[0] == STEPS
                after(dve, g_turned, j)
                nc.vector.tensor_tensor(g[:, 0:NH].rearrange("p (e r) -> p e r", r=RANK),
                                        gm[:, :].rearrange("p (e o) -> p e o", o=1).to_broadcast([P, NEX, RANK]),
                                        ra_ps[:, 0:NH].rearrange("p (e r) -> p e r", r=RANK), ALU.mult).then_inc(g_ready, 1)

            def finish(j, slot):
                dve.wait_ge(o_ready, j + 1)
                after(dve, res_out[slot], (j - slot) * 8)
                nc.vector.tensor_tensor(res[:, slot, :], x1[:, slot, :], o_ps[slot][:, :], ALU.add).then_inc(res_ready, 1)

            def body(j, b, i, slot):
                normalise(j + 1, 1 - slot)
                finish(j, slot)
                choose(j + 1)

            normalise(0, 0)
            choose(0)
            body(0, 0, 0, 0)
            body(1, 0, 0, 1)
            with dve.Fori(1, NT // 2 - 1) as q:
                body(q * 2, 0, 0, 0)
                body(q * 2 + 1, 0, 0, 1)
            body(NT - 2, 0, 0, 0)
            finish(NT - 1, 1)


def program(nc, t, out):
    u_d, delta_d, du_d, sz_d, yy_d = (
        nc.dram_tensor(name, (B, DI, L), FP32, kind="Internal").ap() for name in ("u_d", "delta_d", "du_d", "sz_d", "yy_d"))
    parts_d = nc.dram_tensor("parts_d", (B, 96, L), BF16, kind="Internal").ap()
    front_stage(nc, t["x"], t["ctxT"], t["w_inT"], t["w_xT"], t["w_dtT"], t["chan"], u_d, delta_d, du_d, sz_d, parts_d)
    scan_stage(nc, t["d_chan"], t["a_log"], t["pick"], t["ident"], u_d, delta_d, du_d, sz_d, parts_d, yy_d)
    dense_stage(nc, t["x"], yy_d, t["w_oT"], t["w_raT"], t["w_bT"], t["ident"], t["iota"], out)


def kernel(**inputs):
    import numpy as np
    import concourse.bacc as bacc
    from concourse.bass_utils import run_bass_kernel_spmd as run

    i = {k: np.asarray(v) for k, v in inputs.items()}
    w_x = i["L0_xattn_x_proj_w"]
    bc = w_x[DR:]
    pick = np.zeros((96, 2 * DS, P), np.float32)
    for n in range(2 * DS):
        pick[n::32, n, :] = 1.0
    arrays = {
        "x": i["x"],
        "ctxT": i["ctx_1024"].transpose(0, 2, 1),
        "w_inT": i["L0_xattn_in_proj_w"].T,
        "w_xT": np.concatenate([bc, bc, bc, w_x[:DR]], 0).T,
        "w_dtT": i["L0_xattn_dt_proj_w"].T,
        "chan": np.concatenate([i["L0_xattn_conv_w"], i["L0_xattn_conv_b"][:, None], i["L0_xattn_dt_proj_b"][:, None]], 1),
        "d_chan": i["L0_xattn_D"].reshape(NE, P).T,
        "a_log": i["L0_xattn_A_log"],
        "w_oT": i["L0_ffn_W_base"].T,
        "w_raT": np.concatenate([i["L0_ffn_A_w"].reshape(NEX * RANK, DI), i["L0_ffn_W_router"]], 0).T,
        "w_bT": np.concatenate([i["L0_ffn_B_w"].transpose(0, 2, 1).reshape(NEX * RANK, DI), i["L0_ffn_b_base"][None]], 0),
        "pick": pick.astype(mybir.dt.np(BF16)),
        "ident": np.eye(P, dtype=np.float32),
        "iota": np.tile(np.arange(NEX, dtype=np.float32), (P, 1)),
    }
    nc = bacc.Bacc("TRN2", target_bir_lowering=False, num_devices=1)
    t = {}
    for name, a in arrays.items():
        arrays[name] = a = np.ascontiguousarray(a)
        t[name] = nc.dram_tensor(f"in_{name}", a.shape, mybir.dt.from_np(a.dtype), kind="ExternalInput").ap()
    out = nc.dram_tensor("out", (B, L, DI), FP32, kind="ExternalOutput").ap()
    program(nc, t, out)
    r = run(nc, [{f"in_{name}": a for name, a in arrays.items()}], core_ids=[0])
    return r.results[0]["out"]
```

```python
import concourse.bass as bass
from concourse import mybir
from contextlib import ExitStack

B, L, DM, DI, DS, DR = 4, 1024, 512, 1024, 16, 32
P = 128
NE = DI // P
NK = DM // P
NC = 4
H = 512
NEX, RANK = 8, 8
NT = B * L // P
SCALE = 16.0 / RANK
EPS = 1e-5
CAP = 40.0
FP32, BF16, U32 = mybir.dt.float32, mybir.dt.bfloat16, mybir.dt.uint32
ALU = mybir.AluOpType
ACT = mybir.ActivationFunctionType


def after(engine, semaphore, count):
    if isinstance(count, int) and count <= 0:
        return
    engine.wait_ge(semaphore, count)


def halves():
    return [slice(h * H, (h + 1) * H) for h in range(L // H)]


def front_stage(nc, t_in, skip_d, delta_d, du_d, gate_d, parts_d, c_d):
    x, ctxT = t_in["x"], t_in["ctxT"]
    NV = 4
    with ExitStack() as stack:
        def sb(name, shape, dt=FP32):
            return stack.enter_context(nc.sbuf_tensor(name, shape, dt))

        def sem(name):
            return stack.enter_context(nc.semaphore(name))

        w_in = sb("w_in", [P, NK, DI])
        w_x = sb("w_x", [P, NE, P])
        w_dt = sb("w_dt", [P, DI])
        ch = sb("ch", [P, NE, NC + 3])
        ident = sb("ident1", [P, P])
        ctx = sb("ctx", [P, NK, L])
        xr = sb("xr", [P, NE, L])
        u = sb("u", [P, NE, L])
        conv = sb("conv", [P, 2, L])
        xd = sb("xd", [P, L])
        rest = sb("rest", [96, L])
        parts = sb("parts", [96, L], BF16)
        mid = sb("mid", [96, L], BF16)
        v = sb("v", [P, NV, L])
        ex = sb("ex", [P, NV, L])
        ex1 = sb("ex1", [P, 2, L])
        ln = sb("ln", [P, 2, L])
        delta = sb("delta", [P, 2, L])
        du = sb("du", [P, 2, L])
        gate = sb("gate", [P, L])
        stats = sb("stats", [P, NE, 2, 6])
        mv = sb("mv", [P, NE, 2])
        std = sb("std", [P, NE])
        rstd = sb("rstd", [P, NE])
        nbias = sb("nbias", [P, NE])
        eps = sb("eps1", [P, 1])
        pause = sb("pause1", [P, 2])
        x_ps = [stack.enter_context(nc.psum_tensor(f"x_ps{i}", [P, L], FP32)) for i in range(2)]
        xd_ps = stack.enter_context(nc.psum_tensor("xd_ps", [P, L], FP32))
        v_ps = stack.enter_context(nc.psum_tensor("v_ps", [P, L], FP32))

        weights_in, ctx_in, xr_in = sem("weights_in"), sem("ctx_in"), sem("xr_in")
        x_ready, conv_begun, conv_step, conv_done = sem("x_ready"), sem("conv_begun"), sem("conv_step"), sem("conv_done")
        u_ready, xd_ready, xd_copied = sem("u_ready"), sem("xd_ready"), sem("xd_copied")
        split_step, split_done = sem("split_step"), sem("split_done")
        v_ready, v_copied, arg_ready, ex_ready = sem("v_ready"), sem("v_copied"), sem("arg_ready"), sem("ex_ready")
        ex1_ready, ln_ready, err_ready, sum_ready = sem("ex1_ready"), sem("ln_ready"), sem("err_ready"), sem("sum_ready")
        delta_ready, du_ready, skip_ready = sem("delta_ready"), sem("du_ready"), sem("skip_ready")
        eps_set, stats_ready, mv_ready, std_ready, rstd_ready, nbias_ready, sz_ready = (
            sem(n) for n in ("eps_set", "stats_ready", "mv_ready", "std_ready", "rstd_ready", "nbias_ready", "sz_ready"))
        gate_turned, gate_copied = sem("gate_turned"), sem("gate_copied")
        skip_out, parts_out, c_out, gate_out = sem("skip_out"), sem("parts_out"), sem("c_out"), sem("gate_out")
        delta_out = [sem(f"delta_out{i}") for i in range(2)]
        du_out = [sem(f"du_out{i}") for i in range(2)]

        def batches(engine, body):
            body(0, False)
            with engine.Fori(1, B - 1) as b:
                body(b, False)
            body(B - 1, True)

        def plane(dram, b, t):
            return dram[bass.ds(b, 1), t * P:(t + 1) * P].rearrange("o p l -> (o p) l")

        block = stack.enter_context(nc.Block())

        @block.sync
        def _(sp):
            def load(b):
                after(sp, x_ready, b * NE)
                sp.dma_start(ctx[:, :, :], ctxT[bass.ds(b, 1)].rearrange("o (k p) l -> p (o k) l", p=P)).then_inc(ctx_in, 16)
                after(sp, gate_turned, b * NE)
                sp.dma_start(xr[:, :, :], x[bass.ds(b, 1)].rearrange("o (k p) l -> p (o k) l", p=P)).then_inc(xr_in, 16)

            sp.dma_start(w_in[:, :, :], t_in["w_inT"].rearrange("(k p) e -> p k e", p=P)).then_inc(weights_in, 16)
            load(0)
            sp.dma_start(ch[:, :, :], t_in["chan"].rearrange("(k p) c -> p k c", p=P)).then_inc(weights_in, 16)
            sp.dma_start(w_x[:, :, :], t_in["w_xT"].rearrange("(k p) e -> p k e", p=P)).then_inc(weights_in, 16)
            sp.dma_start(w_dt[96:96 + DR, :], t_in["w_dtT"]).then_inc(weights_in, 16)
            sp.dma_start(ident[:, :], t_in["ident"]).then_inc(weights_in, 16)

            def body(b, last):
                for t in range(NE):
                    sp.wait_ge(gate_copied, b * NE + t + 1)
                    sp.dma_start(plane(gate_d, b, t), gate[:, :]).then_inc(gate_out, 16)
                if not last:
                    load(b + 1)
                sp.wait_ge(xd_copied, b + 1)
                sp.dma_start(c_d[bass.ds(b, 1)].rearrange("o p l -> (o p) l"), xd[DS:2 * DS, :]).then_inc(c_out, 16)
                for t in range(NE + 1):
                    if t == 3:
                        sp.wait_ge(split_done, b + 1)
                        sp.dma_start(parts_d[bass.ds(b, 1)].rearrange("o p l -> (o p) l"), parts[:, :]).then_inc(parts_out, 16)
                    if t < NE:
                        sp.wait_ge(delta_ready, b * NE + t + 1)
                        sp.dma_start(plane(delta_d, b, t), delta[:, t % 2, :]).then_inc(delta_out[t % 2], 16)
                        sp.wait_ge(du_ready, b * NE + t + 1)
                        sp.dma_start(plane(du_d, b, t), du[:, t % 2, :]).then_inc(du_out[t % 2], 16)
                    if t > 0:
                        sp.wait_ge(skip_ready, b * NE + t)
                        sp.dma_start(plane(skip_d, b, t - 1), u[:, t - 1, :]).then_inc(skip_out, 16)
            batches(sp, body)
            sp.wait_ge(gate_out, 16 * B * NE)
            sp.wait_ge(skip_out, 16 * B * NE)
            sp.wait_ge(parts_out, 16 * B)
            sp.wait_ge(c_out, 16 * B)
            for i in range(2):
                sp.wait_ge(delta_out[i], 16 * B * NE // 2)
                sp.wait_ge(du_out[i], 16 * B * NE // 2)

        @block.tensor
        def _(pe):
            pe.wait_ge(weights_in, 80)

            def body(b, last_batch):
                def project(t):
                    if t == 0:
                        pe.wait_ge(ctx_in, b * 16 + 16)
                    after(pe, conv_done, b * NE + t - 1)
                    for hs in halves():
                        for k in range(NK):
                            last = nc.tensor.matmul(x_ps[t % 2][:, hs], w_in[:, k, t * P:(t + 1) * P], ctx[:, k, hs],
                                                    start=(k == 0), stop=(k == NK - 1))
                    last.then_inc(x_ready, 1)

                project(0)
                for t in range(NE):
                    if t + 1 < NE:
                        project(t + 1)
                    pe.wait_ge(sz_ready, b * NE + t + 1)
                    after(pe, gate_copied, b * NE + t)
                    if t == 0:
                        after(pe, v_copied, b * NE)
                    for j in range(NE):
                        last = nc.tensor.transpose(v_ps[:, j * P:(j + 1) * P], xr[:, t, j * P:(j + 1) * P], ident[:, :])
                    last.then_inc(gate_turned, 1)
                    if t == 0:
                        after(pe, xd_copied, b)
                    pe.wait_ge(u_ready, b * NE + t + 1)
                    for hs in halves():
                        last = nc.tensor.matmul(xd_ps[:, hs], w_x[:, t, :], u[:, t, hs], start=(t == 0), stop=(t == NE - 1))
                last.then_inc(xd_ready, 1)
                pe.wait_ge(xd_copied, b + 1)
                for t in range(NE):
                    if t == 0:
                        pe.wait_ge(gate_copied, b * NE + NE)
                    after(pe, v_copied, b * NE + t)
                    for hs in halves():
                        last = nc.tensor.matmul(v_ps[:, hs], w_dt[96:96 + DR, t * P:(t + 1) * P], xd[96:96 + DR, hs], start=True, stop=True)
                    last.then_inc(v_ready, 1)
            batches(pe, body)

        @block.scalar
        def _(act):
            act.wait_ge(weights_in, 80)

            def body(b, last_batch):
                act.wait_ge(mv_ready, b * NE + NE)
                if isinstance(b, int):
                    act.wait_ge(eps_set, 1)
                nc.scalar.activation(std[:, :], mv[:, :, 1], ACT.Sqrt, bias=eps[:, :]).then_inc(std_ready, 1)

                def copy_gate(t):
                    act.wait_ge(gate_turned, b * NE + t + 1)
                    after(act, gate_out, (b * NE + t) * 16)
                    nc.scalar.activation(gate[:, :], v_ps[:, :], ACT.Copy).then_inc(gate_copied, 1)

                for t in range(NE):
                    act.wait_ge(x_ready, b * NE + t + 1)
                    after(act, u_ready, b * NE + t - 1)
                    nc.scalar.activation(conv[:, t % 2, :], x_ps[t % 2][:, :], ACT.Identity, bias=ch[:, t, NC:NC + 1],
                                         scale=ch[:, t, NC - 1:NC]).then_inc(conv_begun, 1)
                    if t == 0:
                        act.wait_ge(nbias_ready, b + 1)
                    nc.scalar.activation(xr[:, t, :], xr[:, t, :], ACT.Silu, bias=nbias[:, t:t + 1],
                                         scale=rstd[:, t:t + 1]).then_inc(sz_ready, 1)
                    if t > 0:
                        copy_gate(t - 1)
                    if t == 0:
                        after(act, skip_out, b * NE * 16)
                    act.wait_ge(conv_done, b * NE + t + 1)
                    nc.scalar.activation(u[:, t, :], conv[:, t % 2, :], ACT.Silu).then_inc(u_ready, 1)
                copy_gate(NE - 1)
                act.wait_ge(xd_ready, b + 1)
                after(act, v_ready, b * NE)
                after(act, split_done, b)
                after(act, c_out, b * 16)
                nc.scalar.activation(xd[:, :], xd_ps[:, :], ACT.Copy).then_inc(xd_copied, 1)

                def take(t):
                    act.wait_ge(v_ready, b * NE + t + 1)
                    after(act, delta_ready, b * NE + t + 1 - NV)
                    nc.scalar.activation(v[:, t % NV, :], v_ps[:, :], ACT.Identity, bias=ch[:, t, NC + 1:NC + 2]).then_inc(v_copied, 1)

                take(0)
                for t in range(NE + 4):
                    if t + 1 < NE:
                        take(t + 1)
                    if t < NE:
                        act.wait_ge(arg_ready, b * NE + t + 1)
                        nc.scalar.activation(ex[:, t % NV, :], ex[:, t % NV, :], ACT.Exp).then_inc(ex_ready, 1)
                    if 0 <= t - 1 < NE:
                        act.wait_ge(ex1_ready, b * NE + t)
                        after(act, delta_ready, b * NE + t - 2)
                        nc.scalar.activation(ln[:, (t - 1) % 2, :], ex1[:, (t - 1) % 2, :], ACT.Ln).then_inc(ln_ready, 1)
                    if 0 <= t - 4:
                        act.wait_ge(du_ready, b * NE + t - 3)
                        nc.scalar.activation(u[:, t - 4, :], u[:, t - 4, :], ACT.Copy, scale=ch[:, t - 4, NC + 2:NC + 3]).then_inc(skip_ready, 1)
            batches(act, body)

        @block.vector
        def _(dve):
            nc.vector.memset(eps[:, :], EPS).then_inc(eps_set, 1)
            dve.wait_ge(weights_in, 80)

            def body(b, last_batch):
                dve.wait_ge(xr_in, b * 16 + 16)
                for t in range(NE):
                    for i, hs in enumerate(halves()):
                        nc.vector.bn_stats(stats[:, t, i, :], xr[:, t, hs]).then_inc(stats_ready, 1)
                after(dve, std_ready, b)
                nc.vector.memset(pause[:, 0:1], 0.0)
                dve.wait_ge(stats_ready, b * 2 * NE + 2 * NE)
                nc.vector.memset(pause[:, 1:2], 0.0)
                for t in range(NE):
                    nc.vector.bn_aggr(mv[:, t, :], stats[:, t, :, :]).then_inc(mv_ready, 1)
                dve.wait_ge(std_ready, b + 1)
                after(dve, sz_ready, b * NE)
                nc.vector.reciprocal(rstd[:, :], std[:, :]).then_inc(rstd_ready, 1)
                dve.wait_ge(rstd_ready, b + 1)
                nc.vector.scalar_tensor_tensor(nbias[:, :], mv[:, :, 0], -1.0, rstd[:, :], ALU.mult, ALU.mult).then_inc(nbias_ready, 1)
                for t in range(NE):
                    dve.wait_ge(conv_begun, b * NE + t + 1)
                    for back in range(1, NC):
                        if back > 1:
                            dve.wait_ge(conv_step, (b * NE + t) * (NC - 2) + back - 1)
                        nc.vector.scalar_tensor_tensor(
                            conv[:, t % 2, back:], x_ps[t % 2][:, 0:L - back], ch[:, t, NC - 1 - back:NC - back],
                            conv[:, t % 2, back:], ALU.mult, ALU.add).then_inc(conv_step if back < NC - 1 else conv_done, 1)
                dve.wait_ge(xd_copied, b + 1)
                after(dve, parts_out, b * 16)
                split = [
                    lambda: nc.vector.tensor_copy(parts[:, :], xd[0:96, :]),
                    lambda: nc.vector.tensor_tensor(rest[:, :], xd[0:96, :], parts[:, :], ALU.subtract),
                    lambda: nc.vector.tensor_copy(mid[:, :], rest[:, :]),
                    lambda: nc.vector.tensor_tensor(rest[:, :], rest[:, :], mid[:, :], ALU.subtract),
                    lambda: nc.vector.tensor_copy(parts[32:64, :], mid[32:64, :]),
                ]

                def split_link(i):
                    split[i]().then_inc(split_step, 1)

                def clamp(t):
                    dve.wait_ge(v_copied, b * NE + t + 1)
                    after(dve, sum_ready, b * NE + t + 1 - NV)
                    nc.vector.tensor_scalar(ex[:, t % NV, :], v[:, t % NV, :], CAP, None, ALU.min).then_inc(arg_ready, 1)

                def one_plus(t):
                    dve.wait_ge(ex_ready, b * NE + t + 1)
                    after(dve, ln_ready, b * NE + t - 1)
                    nc.vector.tensor_scalar(ex1[:, t % 2, :], ex[:, t % NV, :], 1.0, None, ALU.add).then_inc(ex1_ready, 1)
                    dve.wait_ge(ex1_ready, b * NE + t + 1)
                    nc.vector.scalar_tensor_tensor(ex[:, t % NV, :], ex1[:, t % 2, :], -1.0, ex[:, t % NV, :], ALU.add, ALU.subtract).then_inc(err_ready, 1)

                def finish(t):
                    dve.wait_ge(sum_ready, b * NE + t + 1)
                    after(dve, delta_out[t % 2], b * (NE * 8) + t // 2 * 16)
                    after(dve, du_ready, b * NE + t - 1)
                    nc.vector.tensor_tensor(delta[:, t % 2, :], ln[:, t % 2, :], v[:, t % NV, :], ALU.max).then_inc(delta_ready, 1)

                for t in range(NE + 2):
                    if t < NE:
                        clamp(t)
                    if t < len(split):
                        split_link(t)
                    if 1 <= t <= NE:
                        one_plus(t - 1)
                    if t < len(split):
                        dve.wait_ge(split_step, b * len(split) + t + 1)
                    if t == len(split):
                        nc.vector.tensor_copy(parts[64:96, :], rest[64:96, :]).then_inc(split_done, 1)
                    if t >= 2:
                        finish(t - 2)
            batches(dve, body)

        @block.gpsimd
        def _(pool):
            def body(b, last_batch):
                for t in range(NE + 1):
                    if t < NE:
                        pool.wait_ge(ln_ready, b * NE + t + 1)
                        pool.wait_ge(err_ready, b * NE + t + 1)
                        nc.gpsimd.tensor_tensor(ln[:, t % 2, :], ln[:, t % 2, :], ex[:, t % NV, :], ALU.subtract).then_inc(sum_ready, 1)
                    if t > 0:
                        pool.wait_ge(delta_ready, b * NE + t)
                        after(pool, du_out[(t - 1) % 2], b * (NE * 8) + (t - 1) // 2 * 16)
                        nc.gpsimd.tensor_tensor(du[:, (t - 1) % 2, :], delta[:, (t - 1) % 2, :], u[:, t - 1, :], ALU.mult).then_inc(du_ready, 1)
            batches(pool, body)


LATE = 10


class Dense:

    def __init__(self, nc, stack, t_in, yy_d, out):
        def sb(name, shape, dt=FP32):
            return stack.enter_context(nc.sbuf_tensor(name, shape, dt))

        def sem(name):
            return stack.enter_context(nc.semaphore(name))

        NH = self.NH = NEX * RANK
        self.nc, self.t_in, self.yy_d, self.out = nc, t_in, yy_d, out
        self.w_o = sb("w_o", [P, NE, DI])
        self.w_ra = sb("w_ra", [P, NE, NH + NEX])
        self.w_b = sb("w_b", [NH + 1, DI])
        self.ident = sb("ident", [P, P])
        self.iota = sb("iota", [P, NEX])
        self.yyt = sb("yyt", [P, DI])
        self.xt = sb("xt", [P, DI])
        self.x1 = sb("x1", [P, 2, DI])
        self.xn = sb("xn", [P, DI])
        self.xnT = sb("xnT", [P, NE, P])
        self.res = sb("res", [P, 2, H])
        self.stats = sb("stats3", [P, 2, 6])
        self.mv = sb("mv3", [P, 2])
        self.eps, self.std, self.rstd, self.nbias, self.gap, self.egap, self.esum, self.gate1, self.gate2 = (
            sb(n, [P, 1]) for n in ("eps3", "std3", "rstd3", "nbias3", "gap", "egap", "esum", "gate1", "gate2"))
        self.pause = sb("pause3", [P, 2])
        self.hl = sb("hl", [P, NH + NEX])
        self.top = sb("top", [P, 8])
        self.topi = sb("topi", [P, 8], U32)
        self.topf = sb("topf", [P, 8])
        self.mask = sb("mask", [P, 2, NEX])
        self.gm = sb("gm", [P, NEX])
        self.g = sb("g", [P, NH + 1])
        self.gT = sb("gT", [NH + 1, P])
        self.ps = stack.enter_context(nc.psum_tensor("dense_ps", [P, 2, H], FP32))
        (self.weights_in, self.ones_set, self.tile_in, self.x1_ready, self.stats_ready, self.mv_ready, self.std_ready,
         self.rstd_ready, self.nbias_ready, self.xn_ready, self.xn_turned, self.xnT_ready, self.ra_ready, self.hl_ready,
         self.top_ready, self.gap_ready, self.topi_ready, self.topf_ready, self.egap_ready, self.esum_ready, self.gate1_ready,
         self.gate2_ready, self.mask_ready, self.gm_ready, self.g_ready, self.g_turned, self.gT_ready, self.o_ready,
         self.res_ready) = (sem(n) for n in (
             "dense_weights_in", "ones_set", "tile_in", "x1_ready", "stats3_ready", "mv3_ready", "std3_ready",
             "rstd3_ready", "nbias3_ready", "xn_ready", "xn_turned", "xnT_ready", "ra_ready", "hl_ready",
             "top_ready", "gap_ready", "topi_ready", "topf_ready", "egap_ready", "esum_ready", "gate1_ready",
             "gate2_ready", "mask_ready", "gm_ready", "g_ready", "g_turned", "gT_ready", "o_ready", "res_ready"))
        self.res_out = [sem(f"res_out{h}") for h in range(2)]
        self.xr = t_in["x"].rearrange("b (k p) l -> (b k) p l", p=P)
        self.yr = yy_d.rearrange("b (k p) l -> (b k) p l", p=P)
        self.outr = out.rearrange("b (k p) l -> (b k) p l", p=P)

    def load_weights(self, sp):
        t = self.t_in
        sp.dma_start(self.ident[:, :], t["ident"]).then_inc(self.weights_in, 16)
        sp.dma_start(self.iota[:, :], t["iota"]).then_inc(self.weights_in, 16)
        sp.dma_start(self.w_ra[:, :, :], t["w_raT"].rearrange("(k p) n -> p k n", p=P)).then_inc(self.weights_in, 16)
        sp.dma_start(self.w_b[:, :], t["w_bT"]).then_inc(self.weights_in, 16)
        sp.dma_start(self.w_o[:, :, :], t["w_oT"].rearrange("(k p) n -> p k n", p=P)).then_inc(self.weights_in, 16)

    def load_tile(self, sp, j, yy_out, stored):
        after(sp, self.x1_ready, j)
        sp.dma_start(self.xt[:, :], self.xr[bass.ds(j, 1)].rearrange("o p l -> (o p) l")).then_inc(self.tile_in, 16)
        sp.wait_ge(yy_out, stored)
        sp.dma_start(self.yyt[:, :], self.yr[bass.ds(j, 1)].rearrange("o p l -> (o p) l")).then_inc(self.tile_in, 16)

    def store_half(self, sp, j, h):
        sp.wait_ge(self.res_ready, 2 * j + h + 1)
        sp.dma_start(self.outr[bass.ds(j, 1), :, halves()[h]].rearrange("o p l -> (o p) l"), self.res[:, h, :]).then_inc(self.res_out[h], 16)

    def add_x(self, pool, j, slot):
        pool.wait_ge(self.tile_in, 32 * j + 32)
        after(pool, self.res_ready, 2 * j - 2)
        self.nc.gpsimd.tensor_tensor(self.x1[:, slot, :], self.yyt[:, :], self.xt[:, :], ALU.add).then_inc(self.x1_ready, 1)

    def set_constants(self, dve):
        self.nc.vector.memset(self.eps[:, :], EPS).then_inc(self.ones_set, 1)
        self.nc.vector.memset(self.g[:, self.NH:self.NH + 1], 1.0).then_inc(self.ones_set, 1)

    def row_stats(self, dve, j, slot, h):
        if h == 0:
            dve.wait_ge(self.x1_ready, j + 1)
            after(dve, self.mv_ready, j)
        self.nc.vector.bn_stats(self.stats[:, h, :], self.x1[:, slot, halves()[h]]).then_inc(self.stats_ready, 1)

    def mean_var(self, dve, j):
        after(dve, self.std_ready, j)
        after(dve, self.nbias_ready, j)
        dve.wait_ge(self.stats_ready, 2 * j + 2)
        self.nc.vector.memset(self.pause[:, 0:1], 0.0)
        self.nc.vector.bn_aggr(self.mv[:, :], self.stats[:, :, :]).then_inc(self.mv_ready, 1)

    def inverse_std(self, dve, j):
        dve.wait_ge(self.std_ready, j + 1)
        after(dve, self.xn_ready, j)
        self.nc.vector.reciprocal(self.rstd[:, :], self.std[:, :]).then_inc(self.rstd_ready, 1)

    def norm_bias(self, dve, j):
        dve.wait_ge(self.rstd_ready, j + 1)
        self.nc.vector.scalar_tensor_tensor(self.nbias[:, :], self.mv[:, 0:1], -1.0, self.rstd[:, :], ALU.mult, ALU.mult).then_inc(self.nbias_ready, 1)

    def take_routing(self, dve, j):
        dve.wait_ge(self.ra_ready, j + 1)
        after(dve, self.g_ready, j)
        self.nc.vector.tensor_copy(self.hl[:, :], self.ps[:, 0, 0:self.NH + NEX]).then_inc(self.hl_ready, 1)

    def largest(self, dve, j):
        dve.wait_ge(self.hl_ready, j + 1)
        self.nc.vector.memset(self.pause[:, 1:2], 0.0)
        self.nc.vector.max(self.top[:, :], self.hl[:, self.NH:]).then_inc(self.top_ready, 1)

    def logit_gap(self, dve, j):
        dve.wait_ge(self.top_ready, j + 1)
        self.nc.vector.tensor_tensor(self.gap[:, :], self.top[:, 1:2], self.top[:, 0:1], ALU.subtract).then_inc(self.gap_ready, 1)
        self.nc.vector.max_index(self.topi[:, :], self.top[:, :], self.hl[:, self.NH:]).then_inc(self.topi_ready, 1)

    def chosen(self, dve, j):
        dve.wait_ge(self.topi_ready, j + 1)
        self.nc.vector.tensor_copy(self.topf[:, :], self.topi[:, :]).then_inc(self.topf_ready, 1)

    def gate_sum(self, dve, j):
        dve.wait_ge(self.egap_ready, j + 1)
        self.nc.vector.tensor_scalar(self.esum[:, :], self.egap[:, :], 1.0, 1.0 / SCALE, ALU.add, ALU.mult).then_inc(self.esum_ready, 1)

    def first_gate(self, dve, j):
        dve.wait_ge(self.esum_ready, j + 1)
        self.nc.vector.reciprocal(self.gate1[:, :], self.esum[:, :]).then_inc(self.gate1_ready, 1)

    def second_gate(self, dve, j):
        dve.wait_ge(self.gate1_ready, j + 1)
        self.nc.vector.tensor_tensor(self.gate2[:, :], self.gate1[:, :], self.egap[:, :], ALU.mult).then_inc(self.gate2_ready, 1)

    def gate_mask(self, dve, j, i):
        dve.wait_ge(self.topf_ready, j + 1)
        dve.wait_ge(self.gate2_ready, j + 1)
        self.nc.vector.tensor_scalar(self.mask[:, i, :], self.iota[:, :], self.topf[:, i:i + 1], (self.gate1, self.gate2)[i][:, :],
                                     ALU.is_equal, ALU.mult).then_inc(self.mask_ready, 1)

    def gate_row(self, dve, j):
        dve.wait_ge(self.mask_ready, 2 * j + 2)
        self.nc.vector.tensor_tensor(self.gm[:, :], self.mask[:, 0, :], self.mask[:, 1, :], ALU.add).then_inc(self.gm_ready, 1)

    def gated(self, dve, j):
        dve.wait_ge(self.gm_ready, j + 1)
        after(dve, self.g_turned, j)
        self.nc.vector.tensor_tensor(self.g[:, 0:self.NH].rearrange("p (e r) -> p e r", r=RANK),
                                     self.gm[:, :].rearrange("p (e o) -> p e o", o=1).to_broadcast([P, NEX, RANK]),
                                     self.hl[:, 0:self.NH].rearrange("p (e r) -> p e r", r=RANK), ALU.mult).then_inc(self.g_ready, 1)

    def add_residual(self, dve, j, slot, h):
        dve.wait_ge(self.o_ready, 2 * j + h + 1)
        after(dve, self.res_out[h], j * 16)
        self.nc.vector.tensor_tensor(self.res[:, h, :], self.x1[:, slot, halves()[h]], self.ps[:, 1 - h, :], ALU.add).then_inc(self.res_ready, 1)

    def row_std(self, act, j):
        act.wait_ge(self.mv_ready, j + 1)
        after(act, self.rstd_ready, j)
        self.nc.scalar.activation(self.std[:, :], self.mv[:, 1:2], ACT.Sqrt, bias=self.eps[:, :]).then_inc(self.std_ready, 1)

    def normalise(self, act, j, slot):
        act.wait_ge(self.nbias_ready, j + 1)
        after(act, self.xn_turned, 2 * j)
        self.nc.scalar.activation(self.xn[:, :], self.x1[:, slot, :], ACT.Identity, bias=self.nbias[:, :], scale=self.rstd[:, :]).then_inc(self.xn_ready, 1)

    def take_turned(self, act, j, i):
        act.wait_ge(self.xn_turned, 2 * j + i + 1)
        k = (NE // 2) * (1 - i)
        self.nc.scalar.activation(self.xnT[:, k:k + NE // 2, :], self.ps[:, 1 - i, :], ACT.Copy).then_inc(self.xnT_ready, 1)

    def exp_gap(self, act, j):
        act.wait_ge(self.gap_ready, j + 1)
        after(act, self.gate2_ready, j)
        self.nc.scalar.activation(self.egap[:, :], self.gap[:, :], ACT.Exp).then_inc(self.egap_ready, 1)

    def take_gates(self, act, j):
        act.wait_ge(self.g_turned, j + 1)
        self.nc.scalar.activation(self.gT[:, :], self.ps[0:self.NH + 1, 0, 0:P], ACT.Copy).then_inc(self.gT_ready, 1)

    def turn(self, pe, j, i):
        if i == 0:
            pe.wait_ge(self.xn_ready, j + 1)
        after(pe, self.res_ready, 2 * j - 1 + i)
        for c in range(NE // 2):
            k = (NE // 2) * (1 - i) + c
            last = self.nc.tensor.transpose(self.ps[:, 1 - i, c * P:(c + 1) * P], self.xn[:, k * P:(k + 1) * P], self.ident[:, :])
        last.then_inc(self.xn_turned, 1)

    def route(self, pe, j):
        pe.wait_ge(self.xnT_ready, 2 * j + 2)
        for k in range(NE):
            last = self.nc.tensor.matmul(self.ps[:, 0, 0:self.NH + NEX], self.xnT[:, k, :], self.w_ra[:, k, :], start=(k == 0), stop=(k == NE - 1))
        last.then_inc(self.ra_ready, 1)

    def product(self, pe, j, h, k):
        if h == 1 and k == 0:
            pe.wait_ge(self.gT_ready, j + 1)
        self.nc.tensor.matmul(self.ps[:, 1 - h, :], self.xnT[:, k, :], self.w_o[:, k, halves()[h]], start=(k == 0), stop=False)

    def turn_gates(self, pe, j):
        pe.wait_ge(self.g_ready, j + 1)
        self.nc.tensor.transpose(self.ps[0:self.NH + 1, 0, 0:P], self.g[:, :], self.ident[:, :]).then_inc(self.g_turned, 1)

    def experts(self, pe, j, h):
        pe.wait_ge(self.gT_ready, j + 1)
        self.nc.tensor.matmul(self.ps[:, 1 - h, :], self.gT[:, :], self.w_b[:, halves()[h]], start=False, stop=True).then_inc(self.o_ready, 1)


def scan_stage(nc, t_in, skip_d, delta_d, du_d, gate_d, parts_d, c_d, yy_d, out):
    NBLK = B * NE
    FIRST_TAIL = NBLK - LATE
    with ExitStack() as stack:
        def sb(name, shape, dt=FP32):
            return stack.enter_context(nc.sbuf_tensor(name, shape, dt))

        def sem(name):
            return stack.enter_context(nc.semaphore(name))

        d = Dense(nc, stack, t_in, yy_d, out)
        a = sb("a", [P, NBLK, DS])
        sel = sb("sel", [96, DS, P], BF16)
        parts = sb("parts2", [96, 2, L], BF16)
        c_all = sb("c_all", [P, DS, L])
        delta = sb("delta2", [P, 2, L])
        du = sb("du2", [P, 2, L])
        skip = sb("skip", [P, L])
        gate = sb("gate_tile", [P, L])
        decay = sb("decay", [P, 2, L])
        state = sb("state", [P, 2, L])
        prod = sb("prod", [P, 2, L])
        yy = sb("yy", [P, L])
        row = [stack.enter_context(nc.psum_tensor(f"row{i}", [P, L], FP32)) for i in range(2)]
        y_ps = stack.enter_context(nc.psum_tensor("y_ps", [P, L], FP32))

        a_in, sel_in, a_step = sem("a_in"), sem("sel_in"), sem("a_step")
        parts_in = [sem(f"parts_in{i}") for i in range(2)]
        delta_in = [sem(f"delta_in{i}") for i in range(2)]
        du_in = [sem(f"du_in{i}") for i in range(2)]
        c_in = [sem(f"c_in{n}") for n in range(DS)]
        skip_in, gate_in = sem("skip_in"), sem("gate_in")
        b_ready, decay_ready, dbu_ready, scan_done = sem("b_ready"), sem("decay_ready"), sem("dbu_ready"), sem("scan_done")
        prod_ready, skip_used, summed, yy_ready, yy_out = sem("prod_ready"), sem("skip_used"), sem("summed"), sem("yy_ready"), sem("yy_out")

        def blocks(engine, body, apart=()):
            def level(E):
                return 2 if E >= LATE else 1 if E == LATE - 1 else 0

            E = 0
            extra = (lambda E: (E // NE,)) if apart else (lambda E: ())
            apart = {0, LATE - 2, LATE, NBLK - 2} | set(apart)
            while E < NBLK:
                if E in apart:
                    body(E, 0, level(E), *extra(E))
                    body(E + 1, 1, level(E + 1), *extra(E))
                    E += 2
                else:
                    end = min(e for e in apart | {NBLK} if e > E)
                    with engine.Fori(E // 2, end // 2) as q:
                        body(q * 2, 0, level(E), *extra(E))
                        body(q * 2 + 1, 1, level(E), *extra(E))
                    E = end

        batch_ends = [e for b in range(B) for e in (b * NE, b * NE + NE - 2)]

        def rows_of(dram, E):
            return dram.rearrange("b (k p) l -> (b k) p l", p=P)[bass.ds(E, 1)].rearrange("o p l -> (o p) l")

        block = stack.enter_context(nc.Block())

        def tail_tiles(engine, tail):
            with engine.Fori(FIRST_TAIL // 2, NT // 2 - 1) as q:
                tail(q * 2, 0)
                tail(q * 2 + 1, 1)
            tail(NT - 2, 0)
            tail(NT - 1, 1, more=False)

        @block.sync
        def _(sp):
            def load_streams(E, slot, b):
                after(sp, b_ready, E * DS - DS)
                sp.dma_start(parts[:, slot, :], parts_d[b]).then_inc(parts_in[slot], 16)
                after(sp, decay_ready, E * DS - DS)
                sp.dma_start(delta[:, slot, :], rows_of(delta_d, E)).then_inc(delta_in[slot], 16)
                after(sp, dbu_ready, E * DS - DS)
                sp.dma_start(du[:, slot, :], rows_of(du_d, E)).then_inc(du_in[slot], 16)

            def load_skip(E):
                after(sp, skip_used, E)
                sp.dma_start(skip[:, :], rows_of(skip_d, E)).then_inc(skip_in, 16)

            def load_gate(E):
                after(sp, yy_ready, E)
                sp.dma_start(gate[:, :], rows_of(gate_d, E)).then_inc(gate_in, 16)

            def load_c(E, n, b):
                after(sp, prod_ready, E * DS - DS + n + 1)
                sp.dma_start(c_all[:, n, :], c_d[b, n:n + 1, :].to_broadcast([P, L])).then_inc(c_in[n], 16)

            def store_yy(E, b):
                sp.wait_ge(yy_ready, E + 1)
                sp.dma_start(yy_d[b, :, bass.ds((E - b * NE) * P, P)].rearrange("(k p) c -> p k c", p=P),
                             yy[:, :].rearrange("p (k c) -> p k c", c=P)).then_inc(yy_out, 16)

            sp.dma_start(sel[:, :, :], t_in["pick"]).then_inc(sel_in, 16)
            load_streams(0, 0, 0)
            for b in range(B):
                sp.dma_start(a[:, b * NE:(b + 1) * NE, :], t_in["a_log"].rearrange("(k p) n -> p k n", p=P)).then_inc(a_in, 16)
            load_c(0, 0, 0)
            load_c(0, 1, 0)
            d.load_weights(sp)
            load_skip(0)
            for n in range(2, DS):
                load_c(0, n, 0)
            load_gate(0)

            def body(E, slot, beside, b):
                fills = isinstance(E, int) and E % NE == NE - 1 and E + 1 < NBLK
                if not (isinstance(E, int) and E == NBLK - 1):
                    load_streams(E + 1, 1 - slot, (E + 1) // NE if isinstance(E, int) else b)
                if beside == 2 and not (isinstance(E, int) and E == LATE):
                    d.store_half(sp, E - LATE - 1, 1)
                if not (isinstance(E, int) and E == 0):
                    store_yy(E - 1, (E - 1) // NE if isinstance(E, int) else b)
                    load_gate(E)
                if not (isinstance(E, int) and E == NBLK - 1):
                    load_skip(E + 1)
                if beside:
                    d.load_tile(sp, E + 1 - LATE, yy_out, (E - 1) * 16)
                if fills:
                    for n in range(12):
                        load_c(E + 1, n, b + 1)
                if beside == 2:
                    d.store_half(sp, E - LATE, 0)
                if fills:
                    for n in range(12, DS):
                        load_c(E + 1, n, b + 1)
            blocks(sp, body, batch_ends)

            store_yy(NBLK - 1, B - 1)
            d.store_half(sp, FIRST_TAIL - 1, 1)
            def tail(j, slot, more=True):
                if more:
                    d.load_tile(sp, j + 1, yy_out, NBLK * 16)
                d.store_half(sp, j, 0)
                d.store_half(sp, j, 1)
            tail_tiles(sp, tail)
            for h in range(2):
                sp.wait_ge(d.res_out[h], 16 * NT)

        @block.tensor
        def _(pe):
            pe.wait_ge(sel_in, 16)

            def spread(E, slot, n):
                if n == 0:
                    pe.wait_ge(parts_in[slot], (E - slot) * 8 + 16)
                after(pe, scan_done, E * DS + n - 1)
                for hs in halves():
                    last = nc.tensor.matmul(row[n % 2][:, hs], sel[:, n, :], parts[:, slot, hs], start=True, stop=True)
                last.then_inc(b_ready, 1)

            def turn_into_y(source, first, last_one):
                for j in range(NE):
                    last = nc.tensor.matmul(y_ps[:, j * P:(j + 1) * P], source[:, j * P:(j + 1) * P], d.ident[:, :],
                                            start=(first and j % (H // P) == 0), stop=last_one, is_transpose=True, skip_group_check=True)
                return last

            def begin_y(E):
                after(pe, yy_ready, E)
                pe.wait_ge(skip_in, E * 16 + 16)
                turn_into_y(skip, True, False).then_inc(skip_used, 1)

            def add_up(E, n):
                pe.wait_ge(prod_ready, E * DS + n + 1)
                turn_into_y(prod[:, n % 2, :], False, n == DS - 1).then_inc(summed, 1)

            spread(0, 0, 0)

            def body(E, slot, beside):
                j = E - LATE
                for n in range(DS):
                    if n + 1 < DS:
                        spread(E, slot, n + 1)
                    elif not (isinstance(E, int) and E == NBLK - 1):
                        spread(E + 1, 1 - slot, 0)
                    if isinstance(E, int) and E == 0 and n == 0:
                        pe.wait_ge(d.weights_in, 80)
                    if beside == 2:
                        if n < 2:
                            d.turn(pe, j, n)
                        if n == 2:
                            d.route(pe, j)
                        if 3 <= n < 3 + NE:
                            d.product(pe, j, 0, n - 3)
                        if n == 11:
                            d.turn_gates(pe, j)
                        if n == 12:
                            d.experts(pe, j, 0)
                        if n >= 12:
                            d.product(pe, j, 1, 2 * (n - 12))
                            d.product(pe, j, 1, 2 * (n - 12) + 1)
                        if n == 15:
                            d.experts(pe, j, 1)
                    if n == 0:
                        if not (isinstance(E, int) and E == 0):
                            add_up(E - 1, DS - 1)
                    else:
                        if n == 1:
                            begin_y(E)
                        add_up(E, n - 1)
            blocks(pe, body)
            add_up(NBLK - 1, DS - 1)

            def tail(j, slot, more=True):
                d.turn(pe, j, 0)
                d.turn(pe, j, 1)
                d.route(pe, j)
                for k in range(NE):
                    d.product(pe, j, 0, k)
                d.turn_gates(pe, j)
                d.experts(pe, j, 0)
                for k in range(NE):
                    d.product(pe, j, 1, k)
                d.experts(pe, j, 1)
            tail_tiles(pe, tail)

        @block.scalar
        def _(act):
            act.wait_ge(a_in, 16 * B)
            nc.scalar.activation(a[:, :, :], a[:, :, :], ACT.Exp).then_inc(a_step, 1)
            act.wait_ge(a_step, 1)
            nc.scalar.activation(a[:, :, :], a[:, :, :], ACT.Copy, scale=-1.0).then_inc(a_step, 1)
            act.wait_ge(a_step, 2)
            act.wait_ge(d.ones_set, 2)

            def body(E, slot, beside):
                j = E - LATE
                act.wait_ge(delta_in[slot], (E - slot) * 8 + 16)
                for n in range(DS):
                    after(act, scan_done, E * DS + n - 1)
                    scale = a[:, bass.ds(E, 1), n:n + 1].rearrange("p o n -> p (o n)")
                    nc.scalar.activation(decay[:, n % 2, :], delta[:, slot, :], ACT.Exp, scale=scale).then_inc(decay_ready, 1)
                    if beside == 2:
                        if n == 1:
                            d.take_turned(act, j, 0)
                        if n == 3:
                            d.take_turned(act, j, 1)
                        if n == 6:
                            d.exp_gap(act, j)
                        if n == 12:
                            d.take_gates(act, j)
                    if beside:
                        if n == 13:
                            d.row_std(act, j + 1)
                        if n == 15:
                            d.normalise(act, j + 1, 1 - slot)
            blocks(act, body)

            def tail(j, slot, more=True):
                d.take_turned(act, j, 0)
                d.take_turned(act, j, 1)
                d.exp_gap(act, j)
                d.take_gates(act, j)
                if more:
                    d.row_std(act, j + 1)
                    d.normalise(act, j + 1, 1 - slot)
            tail_tiles(act, tail)

        @block.vector
        def _(dve):
            d.set_constants(dve)

            def drive(E, slot, n):
                if n == 0:
                    dve.wait_ge(du_in[slot], (E - slot) * 8 + 16)
                dve.wait_ge(b_ready, E * DS + n + 1)
                nc.vector.tensor_tensor(row[n % 2][:, :], du[:, slot, :], row[n % 2][:, :], ALU.mult).then_inc(dbu_ready, 1)

            def scan(E, n):
                dve.wait_ge(dbu_ready, E * DS + n + 1)
                dve.wait_ge(decay_ready, E * DS + n + 1)
                after(dve, prod_ready, E * DS + n - 1)
                nc.vector.tensor_tensor_scan(state[:, n % 2, :], decay[:, n % 2, :], row[n % 2][:, :], 0.0,
                                             ALU.mult, ALU.add).then_inc(scan_done, 1)

            def gated_y(E):
                dve.wait_ge(summed, E * DS + DS)
                dve.wait_ge(gate_in, E * 16 + 16)
                after(dve, yy_out, E * 16)
                nc.vector.tensor_tensor(yy[:, :], gate[:, :], y_ps[:, :], ALU.mult).then_inc(yy_ready, 1)

            def body(E, slot, beside):
                j = E - LATE
                for n in range(DS):
                    drive(E, slot, n)
                    if n == 1 and not (isinstance(E, int) and E == 0):
                        gated_y(E - 1)
                    if beside == 2:
                        if n == 4:
                            d.largest(dve, j)
                        if n == 5:
                            d.chosen(dve, j)
                        if n == 7:
                            d.gate_sum(dve, j)
                        if n == 8:
                            d.second_gate(dve, j)
                        if n == 9:
                            d.gate_mask(dve, j, 1)
                        if n == 10:
                            d.gated(dve, j)
                    if beside:
                        if n == 11:
                            d.row_stats(dve, j + 1, 1 - slot, 1)
                        if n == 14:
                            d.inverse_std(dve, j + 1)
                    scan(E, n)
                    if beside == 2:
                        if n == 0 and not (isinstance(E, int) and E == LATE):
                            d.add_residual(dve, j - 1, 1 - slot, 1)
                        if n == 3:
                            d.take_routing(dve, j)
                        if n == 4:
                            d.logit_gap(dve, j)
                        if n == 7:
                            d.first_gate(dve, j)
                        if n == 8:
                            d.gate_mask(dve, j, 0)
                        if n == 9:
                            d.gate_row(dve, j)
                        if n == 13:
                            d.add_residual(dve, j, slot, 0)
                    if beside:
                        if n == 10:
                            d.row_stats(dve, j + 1, 1 - slot, 0)
                        if n == 11:
                            d.mean_var(dve, j + 1)
                        if n == 14:
                            d.norm_bias(dve, j + 1)
            blocks(dve, body)
            d.add_residual(dve, FIRST_TAIL - 1, 1, 1)
            gated_y(NBLK - 1)

            def tail(j, slot, more=True):
                if more:
                    d.row_stats(dve, j + 1, 1 - slot, 0)
                    d.row_stats(dve, j + 1, 1 - slot, 1)
                    d.mean_var(dve, j + 1)
                d.take_routing(dve, j)
                d.largest(dve, j)
                d.logit_gap(dve, j)
                d.chosen(dve, j)
                d.gate_sum(dve, j)
                d.first_gate(dve, j)
                d.second_gate(dve, j)
                d.gate_mask(dve, j, 0)
                d.gate_mask(dve, j, 1)
                d.gate_row(dve, j)
                d.gated(dve, j)
                if more:
                    d.inverse_std(dve, j + 1)
                    d.norm_bias(dve, j + 1)
                d.add_residual(dve, j, slot, 0)
                d.add_residual(dve, j, slot, 1)
            tail_tiles(dve, tail)

        @block.gpsimd
        def _(pool):
            def body(E, slot, beside, b):
                for n in range(DS):
                    if isinstance(E, int) and E % NE == 0:
                        pool.wait_ge(c_in[n], b * 16 + 16)
                    pool.wait_ge(scan_done, E * DS + n + 1)
                    after(pool, summed, E * DS + n - 1)
                    nc.gpsimd.tensor_tensor(prod[:, n % 2, :], state[:, n % 2, :], c_all[:, n, :], ALU.mult).then_inc(prod_ready, 1)
                    if beside and n == 7:
                        d.add_x(pool, E - LATE + 1, 1 - slot)
            blocks(pool, body, batch_ends)

            def tail(j, slot, more=True):
                if more:
                    d.add_x(pool, j + 1, 1 - slot)
            tail_tiles(pool, tail)


def program(nc, t, out):
    skip_d, delta_d, du_d, gate_d, yy_d = (
        nc.dram_tensor(name, (B, DI, L), FP32, kind="Internal").ap() for name in ("skip_d", "delta_d", "du_d", "gate_d", "yy_d"))
    parts_d = nc.dram_tensor("parts_d", (B, 96, L), BF16, kind="Internal").ap()
    c_d = nc.dram_tensor("c_d", (B, DS, L), FP32, kind="Internal").ap()
    front_stage(nc, t, skip_d, delta_d, du_d, gate_d, parts_d, c_d)
    scan_stage(nc, t, skip_d, delta_d, du_d, gate_d, parts_d, c_d, yy_d, out)


def kernel(**inputs):
    import numpy as np
    import concourse.bacc as bacc
    from concourse.bass_utils import run_bass_kernel_spmd as run

    i = {k: np.asarray(v) for k, v in inputs.items()}
    w_x = i["L0_xattn_x_proj_w"]
    bc = w_x[DR:]
    pick = np.zeros((96, DS, P), np.float32)
    for n in range(DS):
        pick[n::32, n, :] = 1.0
    arrays = {
        "x": i["x"],
        "ctxT": i["ctx_1024"].transpose(0, 2, 1),
        "w_inT": i["L0_xattn_in_proj_w"].T,
        "w_xT": np.concatenate([bc, bc, bc, w_x[:DR]], 0).T,
        "w_dtT": i["L0_xattn_dt_proj_w"].T,
        "chan": np.concatenate([i["L0_xattn_conv_w"], i["L0_xattn_conv_b"][:, None], i["L0_xattn_dt_proj_b"][:, None],
                                i["L0_xattn_D"][:, None]], 1),
        "a_log": i["L0_xattn_A_log"],
        "w_oT": i["L0_ffn_W_base"].T,
        "w_raT": np.concatenate([i["L0_ffn_A_w"].reshape(NEX * RANK, DI), i["L0_ffn_W_router"]], 0).T,
        "w_bT": np.concatenate([i["L0_ffn_B_w"].transpose(0, 2, 1).reshape(NEX * RANK, DI), i["L0_ffn_b_base"][None]], 0),
        "pick": pick.astype(mybir.dt.np(BF16)),
        "ident": np.eye(P, dtype=np.float32),
        "iota": np.tile(np.arange(NEX, dtype=np.float32), (P, 1)),
    }
    nc = bacc.Bacc("TRN2", target_bir_lowering=False, num_devices=1)
    t = {}
    for name, a in arrays.items():
        arrays[name] = a = np.ascontiguousarray(a)
        t[name] = nc.dram_tensor(f"in_{name}", a.shape, mybir.dt.from_np(a.dtype), kind="ExternalInput").ap()
    out = nc.dram_tensor("out", (B, L, DI), FP32, kind="ExternalOutput").ap()
    program(nc, t, out)
    r = run(nc, [{f"in_{name}": a for name, a in arrays.items()}], core_ids=[0])
    return r.results[0]["out"]
```

```python
import concourse.bass as bass
from concourse import mybir
from collections import namedtuple
from contextlib import ExitStack

B, L, DM, DI, DS, DR = 4, 1024, 512, 1024, 16, 32
P = 128
NE = DI // P
NK = DM // P
NC = 4
H = 512
NEX, RANK = 8, 8
NT = B * L // P
SCALE = 16.0 / RANK
EPS = 1e-5
CAP = 40.0
FP32, BF16, U32 = mybir.dt.float32, mybir.dt.bfloat16, mybir.dt.uint32
ALU = mybir.AluOpType
ACT = mybir.ActivationFunctionType


def after(engine, semaphore, count):
    if isinstance(count, int) and count <= 0:
        return
    engine.wait_ge(semaphore, count)


def halves():
    return [slice(h * H, (h + 1) * H) for h in range(L // H)]


def front_stage(nc, t_in, u_d, delta_d, du_d, gate_d, parts_d, c_d):
    x, ctxT = t_in["x"], t_in["ctxT"]
    NX, NEXP, NLN, NU = 4, 4, 4, 4
    START = [[0, 1], [2, 3], [4], [5, 6], [7], [], [], []]

    START_ALONE = [[s] for s in range(NE)] + [[], [], []]

    def steps(front):
        return NE if front else len(START_ALONE)

    def stage(front, t, late):
        return (START if front else START_ALONE)[t - late] if t >= late else []

    def du_on_vector(front, s):
        return not front and s % 4 == 1

    with ExitStack() as stack:
        def sb(name, shape, dt=FP32):
            return stack.enter_context(nc.sbuf_tensor(name, shape, dt))

        def sem(name):
            return stack.enter_context(nc.semaphore(name))

        w_in = sb("w_in", [P, NK, DI])
        w_x = sb("w_x", [P, NE, P])
        w_dt = sb("w_dt", [P, DI])
        ch = sb("ch", [P, NE, NC + 2])
        ident = sb("ident1", [P, P])
        ctx = sb("ctx", [P, NK, L])
        xr = sb("xr", [P, NX, L])
        u = sb("u", [P, 2, L])
        conv = sb("conv", [P, 2, L])
        gate = sb("gate", [P, 2, L])
        xd = sb("xd", [P, L])
        rest = sb("rest", [96, L])
        parts = sb("parts", [96, L], BF16)
        mid = sb("mid", [96, L], BF16)
        v = sb("v", [P, NE, L])
        ex = sb("ex", [P, NEXP, L])
        ex1 = sb("ex1", [P, 2, L])
        ln = sb("ln", [P, NLN, L])
        u_again = sb("u_again", [P, NU, L])
        delta = sb("delta", [P, 2, L])
        du = sb("du", [P, 2, L])
        stats = sb("stats", [P, 2, 2, 6])
        mv = sb("mv", [P, 2, 2])
        lnvar = sb("lnvar", [P, 2])
        rstd = sb("rstd", [P, 2])
        nbias = sb("nbias", [P, 2])
        eps = sb("eps1", [P, 1])
        pause = sb("pause1", [P, 2])
        x_ps = [stack.enter_context(nc.psum_tensor(f"x_ps{i}", [P, L], FP32)) for i in range(2)]
        xd_ps = stack.enter_context(nc.psum_tensor("xd_ps", [P, L], FP32))
        v_ps = stack.enter_context(nc.psum_tensor("v_ps", [P, L], FP32))

        weights_in = sem("weights_in")
        ctx_in = [sem(f"ctx_in{k}") for k in range(NK)]
        w_in_in = [sem(f"w_in_in{k}") for k in range(NK)]
        xr_in = [sem(f"xr_in{i}") for i in range(NX)]
        ctx_used, x_ready, conv_begun, conv_step, conv_done, u_ready, u_used, xd_copied = (sem(n) for n in (
            "ctx_used", "x_ready", "conv_begun", "conv_step", "conv_done", "u_ready", "u_used", "xd_copied"))
        split_step, split_done = sem("split_step"), sem("split_done")
        v_ready, v_copied, arg_ready, ex_ready, ex1_ready, ln_ready, err_ready, sum_ready, delta_ready = (
            sem(n) for n in ("v_ready", "v_copied", "arg_ready", "ex_ready", "ex1_ready", "ln_ready", "err_ready",
                             "sum_ready", "delta_ready"))
        du_ready = [sem(f"du_ready{i}") for i in range(2)]
        eps_set, stats_ready, mv_ready, lnvar_ready, rstd_ready, nbias_ready, sz_ready, gate_turned, gate_copied = (
            sem(n) for n in ("eps_set", "stats_ready", "mv_ready", "lnvar_ready", "rstd_ready", "nbias_ready",
                             "sz_ready", "gate_turned", "gate_copied"))
        parts_out, c_out = sem("parts_out"), sem("c_out")
        gate_out, u_out, delta_out, du_out = (
            [sem(f"{n}{i}") for i in range(2)] for n in ("gate_out", "u_out", "delta_out", "du_out"))
        u_again_in = [sem(f"u_again_in{i}") for i in range(NU)]

        def batches(engine, body):
            body(0, True, False)
            body(1, True, True)
            with engine.Fori(2, B - 1) as b:
                body(b, True, True)
            body(B - 1, True, True)
            body(B, False, True)

        def ahead(b, t):
            return not isinstance(b, int) or b * NE + t < B * NE

        def rows_of(dram, E):
            return dram.rearrange("b (k p) l -> (b k) p l", p=P)[bass.ds(E, 1)].rearrange("o p l -> (o p) l")

        block = stack.enter_context(nc.Block())

        @block.sync
        def _(sp):
            def load_ctx(b, k):
                if k < NK - 1:
                    after(sp, ctx_used, (b - 1) * (NK - 1) + k + 1)
                else:
                    after(sp, x_ready, b * NE)
                sp.dma_start(ctx[:, k, :], ctxT[bass.ds(b, 1), k * P:(k + 1) * P, :].rearrange("o p l -> (o p) l")).then_inc(ctx_in[k], 16)

            def load_x(E, t):
                after(sp, gate_turned, E - NX + 1)
                sp.dma_start(xr[:, t % NX, :], rows_of(x, E)).then_inc(xr_in[t % NX], 16)

            def store_chain(b, s):
                V = (b - 1) * NE + s
                sp.wait_ge(delta_ready, V + 1)
                sp.dma_start(rows_of(delta_d, V), delta[:, s % 2, :]).then_inc(delta_out[s % 2], 16)
                sp.wait_ge(du_ready[s % 2], (b - 1) * (NE // 2) + s // 2 + 1)
                sp.dma_start(rows_of(du_d, V), du[:, s % 2, :]).then_inc(du_out[s % 2], 16)

            for k in range(NK):
                load_ctx(0, k)
                sp.dma_start(w_in[:, k, :], t_in["w_inT"][k * P:(k + 1) * P, :]).then_inc(w_in_in[k], 16)
                if k == 0:
                    sp.dma_start(ch[:, :, :], t_in["chan"]).then_inc(weights_in, 16)
                    load_x(0, 0)
                    load_x(1, 1)
                    sp.dma_start(ident[:, :], t_in["ident"]).then_inc(weights_in, 16)
            sp.dma_start(w_x[:, :, :], t_in["w_xT"].rearrange("(k p) e -> p k e", p=P)).then_inc(weights_in, 16)
            load_x(2, 2)
            sp.dma_start(w_dt[96:96 + DR, :], t_in["w_dtT"]).then_inc(weights_in, 16)

            def body(b, front, chain):
                for t in range(steps(front)):
                    E = b * NE + t
                    if chain and t == 0:
                        sp.wait_ge(xd_copied, b)
                        sp.dma_start(c_d[bass.ds(b - 1, 1)].rearrange("o p l -> (o p) l"), xd[DS:2 * DS, :]).then_inc(c_out, 16)
                    if front:
                        if ahead(b, t + 3):
                            load_x(E + 3, t + 3)
                    if front and t == NE - 2 and ahead(b, NE):
                        load_ctx(b + 1, 0)
                        load_ctx(b + 1, 1)
                    if chain and t > 0:
                        for s in stage(front, t - 1, 3):
                            store_chain(b, s)
                    if t == 0 and not (isinstance(b, int) and b < 2):
                        for s in stage(True, NE - 1, 3):
                            store_chain(b - 1, s)
                    if chain:
                        for s in stage(front, t, 2):
                            sp.wait_ge(u_out[s % 2], b * (8 * NE))
                            after(sp, du_ready[s % 2], (b - 1) * (NE // 2) + s // 2 - 1)
                            sp.dma_start(u_again[:, s % NU, :], rows_of(u_d, (b - 1) * NE + s)).then_inc(u_again_in[s % NU], 16)
                    if front and t == NE - 2 and ahead(b, NE):
                        load_ctx(b + 1, 2)
                        load_ctx(b + 1, 3)
                    if chain and t == 6:
                        sp.wait_ge(split_done, b)
                        sp.dma_start(parts_d[bass.ds(b - 1, 1)].rearrange("o p l -> (o p) l"), parts[:, :]).then_inc(parts_out, 16)
                if not front:
                    for s in stage(front, steps(front) - 1, 3):
                        store_chain(b, s)
            batches(sp, body)
            for i in range(2):
                for stored in (gate_out, u_out, delta_out, du_out):
                    sp.wait_ge(stored[i], 8 * B * NE)
            sp.wait_ge(parts_out, 16 * B)
            sp.wait_ge(c_out, 16 * B)

        @block.tensor
        def _(pe):
            def project(b, t, slices):
                E, c = b * NE + t, t % NE
                if 0 in slices:
                    after(pe, conv_done, E - 1)
                for k in slices:
                    if c == 0:
                        pe.wait_ge(ctx_in[k], (b + t // NE) * 16 + 16)
                    if isinstance(b, int) and E == 0:
                        pe.wait_ge(w_in_in[k], 16)
                    for hs in halves():
                        last = nc.tensor.matmul(x_ps[t % 2][:, hs], w_in[:, k, c * P:(c + 1) * P], ctx[:, k, hs],
                                                start=(k == 0), stop=(k == NK - 1), skip_group_check=True)
                    if k == NK - 1:
                        last.then_inc(x_ready, 1)
                    elif c == NE - 1:
                        last.then_inc(ctx_used, 1)

            project(0, 0, range(NK))
            pe.wait_ge(weights_in, 64)

            def body(b, front, chain):
                def project_step(s, t):
                    V = (b - 1) * NE + s
                    target = v_ps if front else x_ps[s % 2]
                    if front:
                        pe.wait_ge(gate_copied, b * NE + t + 1)
                        after(pe, v_copied, V)
                    else:
                        after(pe, v_copied, V - 1)
                        pe.wait_ge(conv_done, b * NE)
                    for hs in halves():
                        last = nc.tensor.matmul(target[:, hs], w_dt[96:96 + DR, s * P:(s + 1) * P], xd[96:96 + DR, hs], start=True, stop=True)
                    last.then_inc(v_ready, 1)

                for t in range(steps(front)):
                    E = b * NE + t
                    if front:
                        pe.wait_ge(sz_ready, E + 1)
                        after(pe, gate_copied, E)
                        if chain:
                            after(pe, v_copied, (b - 1) * NE + sum(len(stage(front, i, 0)) for i in range(t)))
                        for j in range(NE):
                            last = nc.tensor.transpose(v_ps[:, j * P:(j + 1) * P], xr[:, t % NX, j * P:(j + 1) * P], ident[:, :])
                        last.then_inc(gate_turned, 1)
                        if ahead(b, t + 1):
                            project(b, t + 1, [0, 1])
                    if chain:
                        if t == 0:
                            pe.wait_ge(xd_copied, b)
                        for s in stage(front, t, 0)[:1]:
                            project_step(s, t)
                    if front:
                        if ahead(b, t + 1):
                            project(b, t + 1, [2, 3])
                        if t == 0:
                            after(pe, xd_copied, b)
                        pe.wait_ge(u_ready, E + 1)
                        for hs in halves():
                            last = nc.tensor.matmul(xd_ps[:, hs], w_x[:, t, :], u[:, t % 2, hs], start=(t == 0), stop=(t == NE - 1),
                                                    skip_group_check=True)
                        last.then_inc(u_used, 1)
                    if chain:
                        for s in stage(front, t, 0)[1:]:
                            project_step(s, t)
            batches(pe, body)

        @block.scalar
        def _(act):
            act.wait_ge(eps_set, 1)

            def inverse_std(E, t):
                act.wait_ge(mv_ready, E + 1)
                nc.scalar.activation(lnvar[:, t % 2:t % 2 + 1], mv[:, t % 2, 1:2], ACT.Ln, bias=eps[:, :]).then_inc(lnvar_ready, 1)
                act.wait_ge(lnvar_ready, E + 1)
                after(act, nbias_ready, E - 1)
                after(act, sz_ready, E - 1)
                nc.scalar.activation(rstd[:, t % 2:t % 2 + 1], lnvar[:, t % 2:t % 2 + 1], ACT.Exp, scale=-0.5).then_inc(rstd_ready, 1)

            def gate_rows(E, t):
                act.wait_ge(nbias_ready, E + 1)
                nc.scalar.activation(xr[:, t % NX, :], xr[:, t % NX, :], ACT.Silu, bias=nbias[:, t % 2:t % 2 + 1],
                                     scale=rstd[:, t % 2:t % 2 + 1]).then_inc(sz_ready, 1)

            nc.scalar.preload_act_table_set("natural_log_exp_and_others")
            inverse_std(0, 0)
            inverse_std(1, 1)
            nc.scalar.preload_act_table_set("silu_and_others")
            gate_rows(0, 0)
            act.wait_ge(weights_in, 64)

            def body(b, front, chain):
                def copy_step(s):
                    source = v_ps if front else x_ps[s % 2]
                    V = (b - 1) * NE + s
                    act.wait_ge(v_ready, V + 1)
                    after(act, delta_ready, V + 1 - NE)
                    nc.scalar.activation(v[:, s, :], source[:, :], ACT.Identity, bias=ch[:, s, NC + 1:NC + 2]).then_inc(v_copied, 1)

                for t in range(steps(front)):
                    E = b * NE + t
                    if chain and t == 0:
                        act.wait_ge(u_used, b * NE)
                        after(act, v_ready, (b - 1) * NE)
                        after(act, split_done, b - 1)
                        after(act, c_out, (b - 1) * 16)
                        nc.scalar.activation(xd[:, :], xd_ps[:, :], ACT.Copy).then_inc(xd_copied, 1)
                    if front:
                        act.wait_ge(x_ready, E + 1)
                        after(act, u_ready, E - 1)
                        nc.scalar.activation(conv[:, t % 2, :], x_ps[t % 2][:, :], ACT.Identity, bias=ch[:, t, NC:NC + 1],
                                             scale=ch[:, t, NC - 1:NC]).then_inc(conv_begun, 1)
                        act.wait_ge(gate_turned, E + 1)
                        after(act, gate_out[t % 2], b * (8 * NE) + t // 2 * 16)
                        nc.scalar.activation(gate[:, t % 2, :], v_ps[:, :], ACT.Copy).then_inc(gate_copied, 1)
                        if ahead(b, t + 1):
                            gate_rows(E + 1, t + 1)
                        act.wait_ge(gate_copied, E + 1)
                        act.dma_start(rows_of(gate_d, E), gate[:, t % 2, :]).then_inc(gate_out[t % 2], 16)
                        act.wait_ge(conv_done, E + 1)
                        after(act, u_out[t % 2], b * (8 * NE) + t // 2 * 16)
                        after(act, u_used, E - 1)
                        nc.scalar.activation(u[:, t % 2, :], conv[:, t % 2, :], ACT.Silu).then_inc(u_ready, 1)
                        nc.scalar.preload_act_table_set("natural_log_exp_and_others")
                    if chain:
                        for s in stage(front, t, 0)[:1]:
                            copy_step(s)
                        for s in stage(front, t, 1):
                            act.wait_ge(arg_ready, (b - 1) * NE + s + 1)
                            nc.scalar.activation(ex[:, s % NEXP, :], ex[:, s % NEXP, :], ACT.Exp).then_inc(ex_ready, 1)
                    if front:
                        if ahead(b, t + 2):
                            inverse_std(E + 2, t + 2)
                        act.wait_ge(u_ready, E + 1)
                        act.dma_start(rows_of(u_d, E), u[:, t % 2, :]).then_inc(u_out[t % 2], 16)
                    if chain:
                        for s in stage(front, t, 0)[1:]:
                            copy_step(s)
                        for s in stage(front, t, 2):
                            V = (b - 1) * NE + s
                            act.wait_ge(ex1_ready, V + 1)
                            after(act, delta_ready, V + 1 - NLN)
                            nc.scalar.activation(ln[:, s % NLN, :], ex1[:, s % 2, :], ACT.Ln).then_inc(ln_ready, 1)
            batches(act, body)

        def make_du(arithmetic, engine, b, s):
            engine.wait_ge(delta_ready, (b - 1) * NE + s + 1)
            engine.wait_ge(u_again_in[s % NU], (b - 1) * (16 * NE // NU) + s // NU * 16 + 16)
            after(engine, du_out[s % 2], (b - 1) * (8 * NE) + s // 2 * 16)
            arithmetic.tensor_tensor(du[:, s % 2, :], delta[:, s % 2, :], u_again[:, s % NU, :], ALU.mult).then_inc(du_ready[s % 2], 1)

        @block.vector
        def _(dve):
            nc.vector.memset(eps[:, :], EPS).then_inc(eps_set, 1)

            def row_stats(E, b, t):
                if isinstance(E, int):
                    dve.wait_ge(xr_in[t % NX], (E // NX + 1) * 16)
                else:
                    dve.wait_ge(xr_in[t % NX], b * (16 * NE // NX) + (t // NX + 1) * 16)
                for i, hs in enumerate(halves()):
                    nc.vector.bn_stats(stats[:, t % 2, i, :], xr[:, t % NX, hs]).then_inc(stats_ready, 1)
                after(dve, lnvar_ready, E - 1)
                after(dve, nbias_ready, E - 1)
                dve.wait_ge(stats_ready, 2 * E + 2)
                nc.vector.memset(pause[:, 0:1], 0.0)
                nc.vector.bn_aggr(mv[:, t % 2, :], stats[:, t % 2, :, :]).then_inc(mv_ready, 1)

            def norm_bias(E, t):
                dve.wait_ge(rstd_ready, E + 1)
                after(dve, sz_ready, E - 1)
                nc.vector.scalar_tensor_tensor(nbias[:, t % 2:t % 2 + 1], mv[:, t % 2, 0:1], -1.0, rstd[:, t % 2:t % 2 + 1],
                                               ALU.mult, ALU.mult).then_inc(nbias_ready, 1)

            row_stats(0, 0, 0)
            row_stats(1, 0, 1)
            norm_bias(0, 0)
            row_stats(2, 0, 2)
            dve.wait_ge(weights_in, 64)

            def body(b, front, chain):
                split = [
                    lambda: nc.vector.tensor_copy(parts[:, :], xd[0:96, :]),
                    lambda: nc.vector.tensor_tensor(rest[:, :], xd[0:96, :], parts[:, :], ALU.subtract),
                    lambda: nc.vector.tensor_copy(mid[:, :], rest[:, :]),
                    lambda: nc.vector.tensor_tensor(rest[:, :], rest[:, :], mid[:, :], ALU.subtract),
                    lambda: nc.vector.tensor_copy(parts[32:64, :], mid[32:64, :]),
                ]

                for t in range(steps(front)):
                    E = b * NE + t
                    if front and ahead(b, t + 1):
                        norm_bias(E + 1, t + 1)
                    if front:
                        dve.wait_ge(conv_begun, E + 1)
                        for back in range(1, NC):
                            if back > 1:
                                dve.wait_ge(conv_step, E * (NC - 2) + back - 1)
                            nc.vector.scalar_tensor_tensor(
                                conv[:, t % 2, back:], x_ps[t % 2][:, 0:L - back], ch[:, t, NC - 1 - back:NC - back],
                                conv[:, t % 2, back:], ALU.mult, ALU.add).then_inc(conv_step if back < NC - 1 else conv_done, 1)
                    if chain:
                        for s in stage(front, t, 1):
                            V = (b - 1) * NE + s
                            dve.wait_ge(v_copied, V + 1)
                            after(dve, sum_ready, V + 1 - NEXP)
                            nc.vector.tensor_scalar(ex[:, s % NEXP, :], v[:, s, :], CAP, None, ALU.min).then_inc(arg_ready, 1)
                    if chain:
                        if t == 0:
                            dve.wait_ge(xd_copied, b)
                            after(dve, parts_out, (b - 1) * 16)
                        if 0 < t <= len(split):
                            dve.wait_ge(split_step, (b - 1) * len(split) + t)
                        if t < len(split):
                            split[t]().then_inc(split_step, 1)
                        if t == len(split):
                            nc.vector.tensor_copy(parts[64:96, :], rest[64:96, :]).then_inc(split_done, 1)
                        for s in stage(front, t, 2):
                            V = (b - 1) * NE + s
                            dve.wait_ge(ex_ready, V + 1)
                            after(dve, ln_ready, V - 1)
                            after(dve, err_ready, V - 1)
                            nc.vector.tensor_scalar(ex1[:, s % 2, :], ex[:, s % NEXP, :], 1.0, None, ALU.add).then_inc(ex1_ready, 1)
                        for s in stage(front, t, 2):
                            V = (b - 1) * NE + s
                            dve.wait_ge(ex1_ready, V + 1)
                            nc.vector.scalar_tensor_tensor(ex[:, s % NEXP, :], ex1[:, s % 2, :], -1.0, ex[:, s % NEXP, :],
                                                           ALU.add, ALU.subtract).then_inc(err_ready, 1)
                        for s in stage(front, t, 3):
                            V = (b - 1) * NE + s
                            dve.wait_ge(sum_ready, V + 1)
                            after(dve, delta_out[s % 2], (b - 1) * (8 * NE) + s // 2 * 16)
                            after(dve, du_ready[s % 2], (b - 1) * (NE // 2) + s // 2)
                            nc.vector.tensor_tensor(delta[:, s % 2, :], ln[:, s % NLN, :], v[:, s, :], ALU.max).then_inc(delta_ready, 1)
                        for s in stage(front, t, 3):
                            if du_on_vector(front, s):
                                make_du(nc.vector, dve, b, s)
                    if front and ahead(b, t + 3):
                        row_stats(E + 3, b, t + 3)
            batches(dve, body)

        @block.gpsimd
        def _(pool):
            def body(b, front, chain):
                if not chain:
                    return
                def less_error(s):
                    V = (b - 1) * NE + s
                    pool.wait_ge(ln_ready, V + 1)
                    pool.wait_ge(err_ready, V + 1)
                    nc.gpsimd.tensor_tensor(ln[:, s % NLN, :], ln[:, s % NLN, :], ex[:, s % NEXP, :], ALU.subtract).then_inc(sum_ready, 1)

                for t in range(steps(front)):
                    for s in [] if front else stage(front, t, 2):
                        less_error(s)
                    for s in stage(front, t, 3):
                        if not du_on_vector(front, s):
                            make_du(nc.gpsimd, pool, b, s)
                    for s in stage(front, t, 2) if front else []:
                        less_error(s)
            batches(pool, body)


Places = namedtuple("Places", "turned routed gates xnT")
LATE = 9


class Dense:

    def __init__(self, nc, stack, t_in, yy_d, out):
        def sb(name, shape, dt=FP32):
            return stack.enter_context(nc.sbuf_tensor(name, shape, dt))

        def sem(name):
            return stack.enter_context(nc.semaphore(name))

        NH = self.NH = NEX * RANK
        self.nc, self.t_in, self.yy_d, self.out = nc, t_in, yy_d, out
        self.w_o = sb("w_o", [P, NE, DI])
        self.w_ra = sb("w_ra", [P, NE, NH + NEX])
        self.w_b = sb("w_b", [NH + 1, DI])
        self.ident = sb("ident", [P, P])
        self.iota = sb("iota", [P, NEX])
        self.yyt = sb("yyt", [P, DI])
        self.xt = sb("xt", [P, DI])
        self.x1 = sb("x1", [P, 2, DI])
        self.xn = sb("xn", [P, DI])
        self.xnT = sb("xnT", [P, 2, NE, P])
        self.res = sb("res", [P, 2, H])
        (self.eps, self.unit, self.rowsum, self.nmean, self.sumsq, self.lnvar, self.rstd, self.nbias, self.egap, self.esum,
         self.gate1, self.gate2) = (sb(n, [P, 1]) for n in (
             "eps3", "unit", "rowsum", "nmean", "sumsq", "lnvar3", "rstd3", "nbias3", "egap", "esum", "gate1", "gate2"))
        self.pause = sb("pause3", [P, 1])
        self.hl = sb("hl", [P, NH + NEX])
        self.top = sb("top", [P, 8])
        self.topi = sb("topi", [P, 8], U32)
        self.topf = sb("topf", [P, 8])
        self.mask = sb("mask", [P, 2, NEX])
        self.gm = sb("gm", [P, NEX])
        self.g = sb("g", [P, NH + 1])
        self.gT = sb("gT", [NH + 1, P])
        self.ps = stack.enter_context(nc.psum_tensor("dense_ps", [P, 2, H], FP32))
        self.beside = [Places((self.ps[:, 1, :], self.ps[:, 1, :]), self.ps[:, 1, 0:NH + NEX], self.ps[0:NH + 1, 0, 0:P], self.xnT[:, slot])
                       for slot in range(2)]
        (self.ident_in, self.weights_in, self.ones_set, self.tile_in, self.x1_ready, self.rowsum_ready,
         self.nmean_ready, self.sumsq_ready, self.lnvar_ready, self.rstd_ready, self.nbias_ready, self.xn_ready,
         self.xn_turned, self.xnT_ready, self.ra_ready, self.hl_ready, self.top_ready, self.topi_ready,
         self.topf_ready, self.egap_ready, self.esum_ready, self.gate1_ready, self.gate2_ready, self.mask_ready,
         self.gm_ready, self.g_ready, self.g_turned, self.gT_ready, self.o_ready, self.res_ready) = (
            sem(n) for n in (
                "ident_in", "dense_weights_in", "ones_set", "tile_in", "x1_ready", "rowsum_ready", "nmean_ready",
                "sumsq_ready", "lnvar3_ready", "rstd3_ready", "nbias3_ready", "xn_ready", "xn_turned", "xnT_ready",
                "ra_ready", "hl_ready", "top_ready", "topi_ready", "topf_ready", "egap_ready", "esum_ready",
                "gate1_ready", "gate2_ready", "mask_ready", "gm_ready", "g_ready", "g_turned", "gT_ready", "o_ready",
                "res_ready"))
        self.res_out = [sem(f"res_out{h}") for h in range(2)]
        self.xr = t_in["x"].rearrange("b (k p) l -> (b k) p l", p=P)
        self.yr = yy_d.rearrange("b (k p) l -> (b k) p l", p=P)
        self.outr = out.rearrange("b (k p) l -> (b k) p l", p=P)

    def load_weights(self, sp):
        t = self.t_in
        sp.dma_start(self.iota[:, :], t["iota"]).then_inc(self.weights_in, 16)
        sp.dma_start(self.w_ra[:, :, :], t["w_raT"].rearrange("(k p) n -> p k n", p=P)).then_inc(self.weights_in, 16)
        sp.dma_start(self.w_b[:, :], t["w_bT"]).then_inc(self.weights_in, 16)
        sp.dma_start(self.w_o[:, :, :], t["w_oT"].rearrange("(k p) n -> p k n", p=P)).then_inc(self.weights_in, 16)

    def load_tile(self, sp, j, yy_out, stored):
        after(sp, self.x1_ready, 2 * j)
        sp.dma_start(self.xt[:, :], self.xr[bass.ds(j, 1)].rearrange("o p l -> (o p) l")).then_inc(self.tile_in, 16)
        sp.wait_ge(yy_out, stored)
        sp.dma_start(self.yyt[:, :], self.yr[bass.ds(j, 1)].rearrange("o p l -> (o p) l")).then_inc(self.tile_in, 16)

    def store_half(self, sp, j, h):
        sp.wait_ge(self.res_ready, 2 * j + h + 1)
        sp.dma_start(self.outr[bass.ds(j, 1), :, halves()[h]].rearrange("o p l -> (o p) l"), self.res[:, h, :]).then_inc(self.res_out[h], 16)

    def add_x(self, pool, j, slot, h):
        if h == 0:
            pool.wait_ge(self.tile_in, 32 * j + 32)
            after(pool, self.res_ready, 2 * j - 2)
        hs = halves()[h]
        self.nc.gpsimd.tensor_tensor(self.x1[:, slot, hs], self.yyt[:, hs], self.xt[:, hs], ALU.add).then_inc(self.x1_ready, 1)

    def set_constants(self, dve):
        self.nc.vector.memset(self.eps[:, :], EPS).then_inc(self.ones_set, 1)
        self.nc.vector.memset(self.unit[:, :], 1.0 / SCALE).then_inc(self.ones_set, 1)
        self.nc.vector.memset(self.g[:, self.NH:self.NH + 1], 1.0).then_inc(self.ones_set, 1)

    def largest(self, dve, j):
        dve.wait_ge(self.hl_ready, j + 1)
        self.nc.vector.memset(self.pause[:, :], 0.0)
        self.nc.vector.max(self.top[:, :], self.hl[:, self.NH:]).then_inc(self.top_ready, 1)

    def chosen(self, dve, j):
        dve.wait_ge(self.top_ready, j + 1)
        self.nc.vector.memset(self.pause[:, :], 0.0)
        self.nc.vector.max_index(self.topi[:, :], self.top[:, :], self.hl[:, self.NH:]).then_inc(self.topi_ready, 1)

    def first_gate(self, dve, j):
        dve.wait_ge(self.esum_ready, j + 1)
        self.nc.vector.reciprocal(self.gate1[:, :], self.esum[:, :]).then_inc(self.gate1_ready, 1)

    def gate_mask(self, dve, j, i):
        dve.wait_ge(self.topf_ready, j + 1)
        dve.wait_ge(self.gate2_ready, j + 1)
        self.nc.vector.tensor_scalar(self.mask[:, i, :], self.iota[:, :], self.topf[:, i:i + 1], (self.gate1, self.gate2)[i][:, :],
                                     ALU.is_equal, ALU.mult).then_inc(self.mask_ready, 1)

    def gate_row(self, dve, j):
        dve.wait_ge(self.mask_ready, 2 * j + 2)
        self.nc.vector.tensor_tensor(self.gm[:, :], self.mask[:, 0, :], self.mask[:, 1, :], ALU.add).then_inc(self.gm_ready, 1)

    def gated(self, dve, j):
        dve.wait_ge(self.gm_ready, j + 1)
        after(dve, self.g_turned, j)
        self.nc.vector.tensor_tensor(self.g[:, 0:self.NH].rearrange("p (e r) -> p e r", r=RANK),
                                     self.gm[:, :].rearrange("p (e o) -> p e o", o=1).to_broadcast([P, NEX, RANK]),
                                     self.hl[:, 0:self.NH].rearrange("p (e r) -> p e r", r=RANK), ALU.mult).then_inc(self.g_ready, 1)

    def add_residual(self, dve, j, slot, h):
        dve.wait_ge(self.o_ready, 2 * j + h + 1)
        after(dve, self.res_out[h], j * 16)
        self.nc.vector.tensor_tensor(self.res[:, h, :], self.x1[:, slot, halves()[h]], self.ps[:, 1 - h, :], ALU.add).then_inc(self.res_ready, 1)

    def row_sum(self, act, j, slot):
        act.wait_ge(self.x1_ready, 2 * j + 2)
        after(act, self.xn_turned, 2 * j)
        after(act, self.nmean_ready, j)
        self.nc.scalar.activation(self.xn[:, :], self.x1[:, slot, :], ACT.Copy, accum_out=self.rowsum[:, :]).then_inc(self.rowsum_ready, 1)

    def negative_mean(self, act, j):
        act.wait_ge(self.rowsum_ready, j + 1)
        after(act, self.xn_ready, j)
        self.nc.scalar.activation(self.nmean[:, :], self.rowsum[:, :], ACT.Copy, scale=-1.0 / DI).then_inc(self.nmean_ready, 1)

    def squares(self, act, j, slot):
        act.wait_ge(self.nmean_ready, j + 1)
        self.nc.scalar.activation(self.xn[:, :], self.x1[:, slot, :], ACT.Square, bias=self.nmean[:, :],
                                  accum_out=self.sumsq[:, :]).then_inc(self.sumsq_ready, 1)

    def inverse_std(self, act, j):
        act.wait_ge(self.sumsq_ready, j + 1)
        self.nc.scalar.activation(self.lnvar[:, :], self.sumsq[:, :], ACT.Ln, bias=self.eps[:, :], scale=1.0 / DI).then_inc(self.lnvar_ready, 1)
        act.wait_ge(self.lnvar_ready, j + 1)
        self.nc.scalar.activation(self.rstd[:, :], self.lnvar[:, :], ACT.Exp, scale=-0.5).then_inc(self.rstd_ready, 1)

    def norm_bias(self, act, j):
        act.wait_ge(self.rstd_ready, j + 1)
        self.nc.scalar.activation(self.nbias[:, :], self.nmean[:, :], ACT.Copy, scale=self.rstd[:, :]).then_inc(self.nbias_ready, 1)

    def normalise(self, act, j, slot):
        act.wait_ge(self.nbias_ready, j + 1)
        self.nc.scalar.activation(self.xn[:, :], self.x1[:, slot, :], ACT.Identity, bias=self.nbias[:, :], scale=self.rstd[:, :]).then_inc(self.xn_ready, 1)

    def take_routing(self, act, j, at):
        act.wait_ge(self.ra_ready, j + 1)
        after(act, self.g_ready, j)
        self.nc.scalar.activation(self.hl[:, :], at.routed, ACT.Copy).then_inc(self.hl_ready, 1)

    def exp_gap(self, act, j):
        act.wait_ge(self.top_ready, j + 1)
        after(act, self.gate2_ready, j)
        self.nc.scalar.activation(self.egap[:, :], self.top[:, 0:1], ACT.Exp, bias=self.top[:, 1:2], scale=-1.0).then_inc(self.egap_ready, 1)
        act.wait_ge(self.egap_ready, j + 1)
        after(act, self.gate1_ready, j)
        self.nc.scalar.activation(self.esum[:, :], self.egap[:, :], ACT.Identity, bias=self.unit[:, :], scale=1.0 / SCALE).then_inc(self.esum_ready, 1)

    def index_float(self, act, j):
        act.wait_ge(self.topi_ready, j + 1)
        after(act, self.mask_ready, 2 * j)
        self.nc.scalar.activation(self.topf[:, :], self.topi[:, :], ACT.Copy).then_inc(self.topf_ready, 1)

    def second_gate(self, act, j):
        act.wait_ge(self.gate1_ready, j + 1)
        self.nc.scalar.activation(self.gate2[:, :], self.egap[:, :], ACT.Copy, scale=self.gate1[:, :]).then_inc(self.gate2_ready, 1)

    def take_turned(self, act, j, i, at, alone=False):
        act.wait_ge(self.xn_turned, 2 * j + i + 1)
        if alone:
            act.wait_ge(self.o_ready, 2 * j - 2)
        k = (NE // 2) * (1 - i)
        self.nc.scalar.activation(at.xnT[:, k:k + NE // 2, :], at.turned[i], ACT.Copy).then_inc(self.xnT_ready, 1)

    def take_gates(self, act, j, at):
        act.wait_ge(self.g_turned, j + 1)
        self.nc.scalar.activation(self.gT[:, :], at.gates, ACT.Copy).then_inc(self.gT_ready, 1)

    def turn(self, pe, j, i, at, alone=False):
        if i == 0:
            pe.wait_ge(self.xn_ready, j + 1)
        if alone:
            pe.wait_ge(self.xnT_ready, 2 * j - 1 + i)
        elif i == 0:
            after(pe, self.res_ready, 2 * j - 1)
        else:
            pe.wait_ge(self.xnT_ready, 2 * j + 1)
        for c in range(NE // 2):
            k = (NE // 2) * (1 - i) + c
            last = self.nc.tensor.transpose(at.turned[i][:, c * P:(c + 1) * P], self.xn[:, k * P:(k + 1) * P], self.ident[:, :])
        last.then_inc(self.xn_turned, 1)

    def route(self, pe, j, at, alone=False):
        pe.wait_ge(self.xnT_ready, 2 * j + 2)
        if alone:
            pe.wait_ge(self.hl_ready, j)
        for k in range(NE):
            last = self.nc.tensor.matmul(at.routed, at.xnT[:, k, :], self.w_ra[:, k, :], start=(k == 0), stop=(k == NE - 1))
        last.then_inc(self.ra_ready, 1)

    def product(self, pe, j, h, k, at, alone=False):
        if k == 0 and alone:
            pe.wait_ge(self.res_ready, 2 * j - 1 + h)
        elif k == 0 and h == 1:
            pe.wait_ge(self.gT_ready, j + 1)
        elif k == 0:
            pe.wait_ge(self.hl_ready, j + 1)
        self.nc.tensor.matmul(self.ps[:, 1 - h, :], at.xnT[:, k, :], self.w_o[:, k, halves()[h]], start=(k == 0), stop=False)

    def turn_gates(self, pe, j, at, alone=False):
        pe.wait_ge(self.g_ready, j + 1)
        if not alone:
            after(pe, self.res_ready, 2 * j)
        self.nc.tensor.transpose(at.gates, self.g[:, :], self.ident[:, :]).then_inc(self.g_turned, 1)

    def experts(self, pe, j, h):
        pe.wait_ge(self.gT_ready, j + 1)
        self.nc.tensor.matmul(self.ps[:, 1 - h, :], self.gT[:, :], self.w_b[:, halves()[h]], start=False, stop=True).then_inc(self.o_ready, 1)


def scan_stage(nc, t_in, u_d, delta_d, du_d, gate_d, parts_d, c_d, yy_d, out):
    NBLK = B * NE
    FIRST_TAIL = NBLK - LATE
    with ExitStack() as stack:
        def sb(name, shape, dt=FP32):
            return stack.enter_context(nc.sbuf_tensor(name, shape, dt))

        def sem(name):
            return stack.enter_context(nc.semaphore(name))

        d = Dense(nc, stack, t_in, yy_d, out)
        a = sb("a", [P, NBLK, DS + 1])
        sel = sb("sel", [96, DS, P], BF16)
        parts = sb("parts2", [96, 2, L], BF16)
        c_all = sb("c_all", [P, DS, L])
        delta = sb("delta2", [P, 2, L])
        du = sb("du2", [P, 2, L])
        skip = sb("skip", [P, L])
        gate = sb("gate_tile", [P, L])
        decay = sb("decay", [P, 2, L])
        state = sb("state", [P, 2, L])
        prod = sb("prod", [P, 2, L])
        yy = sb("yy", [P, L])
        row = [stack.enter_context(nc.psum_tensor(f"row{i}", [P, L], FP32)) for i in range(2)]
        y_ps = stack.enter_context(nc.psum_tensor("y_ps", [P, L], FP32))

        NHX = d.NH + NEX
        alone = [Places((row[0][:, 0:H], row[0][:, H:L]), row[1][:, 0:NHX], row[1][0:d.NH + 1, H:H + P], d.xnT[:, slot]) for slot in range(2)]

        a_in, sel_in, a_step = sem("a_in"), sem("sel_in"), sem("a_step")
        parts_in = [sem(f"parts_in{i}") for i in range(2)]
        delta_in = [sem(f"delta_in{i}") for i in range(2)]
        du_in = [sem(f"du_in{i}") for i in range(2)]
        c_in = [sem(f"c_in{n}") for n in range(DS)]
        u_in, skip_ready, gate_in = sem("u_in"), sem("skip_ready"), sem("gate_in")
        b_ready, decay_ready, dbu_ready, scan_done = sem("b_ready"), sem("decay_ready"), sem("dbu_ready"), sem("scan_done")
        prod_ready, skip_used, summed, yy_ready, yy_out = sem("prod_ready"), sem("skip_used"), sem("summed"), sem("yy_ready"), sem("yy_out")

        def blocks(engine, body, apart=()):
            def level(E):
                return 2 if E >= LATE else 1 if E == LATE - 1 else 0

            E = 0
            extra = (lambda E: (E // NE,)) if apart else (lambda E: ())
            apart = {0, LATE - 1, NBLK - 2} | set(apart)
            while E < NBLK:
                if E in apart:
                    body(E, 0, level(E), *extra(E))
                    body(E + 1, 1, level(E + 1), *extra(E))
                    E += 2
                else:
                    end = min(e for e in apart | {NBLK} if e > E)
                    with engine.Fori(E // 2, end // 2) as q:
                        body(q * 2, 0, level(E), *extra(E))
                        body(q * 2 + 1, 1, level(E), *extra(E))
                    E = end

        batch_ends = [e for b in range(B) for e in (b * NE, b * NE + NE - 2)]

        def rows_of(dram, E):
            return dram.rearrange("b (k p) l -> (b k) p l", p=P)[bass.ds(E, 1)].rearrange("o p l -> (o p) l")

        block = stack.enter_context(nc.Block())

        def tail_tiles(engine, tail):
            with engine.Fori(0, (LATE - 3) // 2) as q:
                tail(q * 2 + FIRST_TAIL, 0)
                tail(q * 2 + (FIRST_TAIL + 1), 1)
            tail(NT - 3, 0)
            tail(NT - 2, 1, more=1)
            tail(NT - 1, 0, more=0)

        @block.sync
        def _(sp):
            def load_streams(E, slot, b):
                after(sp, b_ready, E * DS - DS)
                sp.dma_start(parts[:, slot, :], parts_d[b]).then_inc(parts_in[slot], 16)
                after(sp, decay_ready, E * DS - DS)
                sp.dma_start(delta[:, slot, :], rows_of(delta_d, E)).then_inc(delta_in[slot], 16)
                after(sp, dbu_ready, E * DS - DS)
                sp.dma_start(du[:, slot, :], rows_of(du_d, E)).then_inc(du_in[slot], 16)

            def load_skip(E):
                after(sp, skip_used, E)
                sp.dma_start(skip[:, :], rows_of(u_d, E)).then_inc(u_in, 16)

            def load_gate(E):
                after(sp, yy_ready, E)
                sp.dma_start(gate[:, :], rows_of(gate_d, E)).then_inc(gate_in, 16)

            def load_c(E, n, b):
                after(sp, prod_ready, E * DS - DS + n + 1)
                sp.dma_start(c_all[:, n, :], c_d[b, n:n + 1, :].to_broadcast([P, L])).then_inc(c_in[n], 16)

            def store_yy(E, b):
                sp.wait_ge(yy_ready, E + 1)
                sp.dma_start(yy_d[b, :, bass.ds((E - b * NE) * P, P)].rearrange("(k p) c -> p k c", p=P),
                             yy[:, :].rearrange("p (k c) -> p k c", c=P)).then_inc(yy_out, 16)

            sp.dma_start(a[:, :, :], t_in["a_log"]).then_inc(a_in, 16)
            sp.dma_start(sel[:, :, :], t_in["pick"]).then_inc(sel_in, 16)
            load_streams(0, 0, 0)
            load_c(0, 0, 0)
            load_c(0, 1, 0)
            load_skip(0)
            sp.dma_start(d.ident[:, :], t_in["ident"]).then_inc(d.ident_in, 16)
            for n in range(2, DS):
                load_c(0, n, 0)
            load_gate(0)

            def body(E, slot, beside, b):
                fills = isinstance(E, int) and E % NE == NE - 1 and E + 1 < NBLK
                if not (isinstance(E, int) and E == NBLK - 1):
                    load_streams(E + 1, 1 - slot, (E + 1) // NE if isinstance(E, int) else b)
                if not (isinstance(E, int) and E == 0):
                    store_yy(E - 1, (E - 1) // NE if isinstance(E, int) else b)
                    load_gate(E)
                if isinstance(E, int) and E == 1:
                    d.load_weights(sp)
                if beside:
                    begins = isinstance(E, int) and E % NE == 0
                    d.load_tile(sp, E + 1 - LATE, yy_out, E * 16 if begins else (E - 1) * 16)
                if beside == 2 and not (isinstance(E, int) and E == LATE):
                    d.store_half(sp, E - LATE - 1, 1)
                if not (isinstance(E, int) and E == NBLK - 1):
                    load_skip(E + 1)
                if fills:
                    for n in range(12):
                        load_c(E + 1, n, b + 1)
                if beside == 2:
                    d.store_half(sp, E - LATE, 0)
                if fills:
                    for n in range(12, DS):
                        load_c(E + 1, n, b + 1)
            blocks(sp, body, batch_ends)

            store_yy(NBLK - 1, B - 1)
            d.load_tile(sp, FIRST_TAIL + 1, yy_out, NBLK * 16)
            d.store_half(sp, FIRST_TAIL - 1, 1)
            def tail(j, slot, more=2):
                if more == 2:
                    d.load_tile(sp, j + 2, yy_out, NBLK * 16)
                d.store_half(sp, j, 0)
                d.store_half(sp, j, 1)
            tail_tiles(sp, tail)
            for h in range(2):
                sp.wait_ge(d.res_out[h], 16 * NT)

        @block.tensor
        def _(pe):
            pe.wait_ge(sel_in, 16)

            def spread(E, slot, n):
                if n == 0:
                    pe.wait_ge(parts_in[slot], (E - slot) * 8 + 16)
                after(pe, scan_done, E * DS + n - 1)
                for hs in halves():
                    last = nc.tensor.matmul(row[n % 2][:, hs], sel[:, n, :], parts[:, slot, hs], start=True, stop=True)
                last.then_inc(b_ready, 1)

            def turn_into_y(source, first, last_one):
                for j in range(NE):
                    last = nc.tensor.matmul(y_ps[:, j * P:(j + 1) * P], source[:, j * P:(j + 1) * P], d.ident[:, :],
                                            start=(first and j % (H // P) == 0), stop=last_one, is_transpose=True, skip_group_check=True)
                return last

            def add_skip(E):
                pe.wait_ge(skip_ready, E + 1)
                turn_into_y(skip, False, False).then_inc(skip_used, 1)

            def add_up(E, n):
                if n == 0:
                    after(pe, yy_ready, E)
                pe.wait_ge(prod_ready, E * DS + n + 1)
                turn_into_y(prod[:, n % 2, :], n == 0, n == DS - 1).then_inc(summed, 1)

            spread(0, 0, 0)

            def body(E, slot, beside):
                j, here = E - LATE, d.beside[slot]
                for n in range(DS):
                    if n + 1 < DS:
                        spread(E, slot, n + 1)
                    elif not (isinstance(E, int) and E == NBLK - 1):
                        spread(E + 1, 1 - slot, 0)
                    if isinstance(E, int) and E == 0 and n == 0:
                        pe.wait_ge(d.ident_in, 16)
                    if isinstance(E, int) and E == LATE and n == 0:
                        pe.wait_ge(d.weights_in, 64)
                    if n >= 2:
                        add_up(E, n - 2)
                        if n == 6:
                            add_skip(E)
                    elif not (isinstance(E, int) and E == 0):
                        add_up(E - 1, DS - 2 + n)
                    if beside == 2:
                        before = not (isinstance(E, int) and E == LATE)
                        if n < NE // 2 and before:
                            d.product(pe, j - 1, 1, n + NE // 2, d.beside[1 - slot])
                        if n == 0:
                            d.turn(pe, j, 0, here)
                        if n == 2:
                            d.turn(pe, j, 1, here)
                        if n == 3 and before:
                            d.experts(pe, j - 1, 1)
                        if n == 4:
                            d.route(pe, j, here)
                        if 5 <= n < 5 + NE:
                            d.product(pe, j, 0, n - 5, here)
                        if n == 10:
                            d.turn_gates(pe, j, here)
                        if n >= DS - NE // 2:
                            d.product(pe, j, 1, n - (DS - NE // 2), here)
                        if n == 13:
                            d.experts(pe, j, 0)
            blocks(pe, body)
            add_up(NBLK - 1, DS - 2)
            add_up(NBLK - 1, DS - 1)
            for k in range(NE // 2, NE):
                d.product(pe, FIRST_TAIL - 1, 1, k, d.beside[1])
            d.experts(pe, FIRST_TAIL - 1, 1)

            pe.wait_ge(scan_done, NBLK * DS)
            for i in range(2):
                d.turn(pe, FIRST_TAIL, i, alone[0], True)
            d.route(pe, FIRST_TAIL, alone[0], True)

            def tail(j, slot, more=2):
                here, then = alone[slot], alone[1 - slot]
                for k in range(NE):
                    d.product(pe, j, 0, k, here, True)
                d.turn_gates(pe, j, here, True)
                for k in range(3):
                    d.product(pe, j, 1, k, here, True)
                d.experts(pe, j, 0)
                if more:
                    d.turn(pe, j + 1, 0, then, True)
                    d.turn(pe, j + 1, 1, then, True)
                for k in range(3, 6):
                    d.product(pe, j, 1, k, here, True)
                if more:
                    d.route(pe, j + 1, then, True)
                for k in range(6, NE):
                    d.product(pe, j, 1, k, here, True)
                d.experts(pe, j, 1)
            tail_tiles(pe, tail)

        @block.scalar
        def _(act):
            nc.scalar.preload_act_table_set("natural_log_exp_and_others")
            act.wait_ge(a_in, 16)
            nc.scalar.activation(a[:, :, 0:DS], a[:, :, 0:DS], ACT.Exp).then_inc(a_step, 1)
            act.wait_ge(a_step, 1)
            nc.scalar.activation(a[:, :, 0:DS], a[:, :, 0:DS], ACT.Copy, scale=-1.0).then_inc(a_step, 1)
            act.wait_ge(a_step, 2)
            act.wait_ge(d.ones_set, 3)

            def scale_skip(E):
                act.wait_ge(u_in, E * 16 + 16)
                scale = a[:, bass.ds(E, 1), DS:DS + 1].rearrange("p o n -> p (o n)")
                nc.scalar.activation(skip[:, :], skip[:, :], ACT.Copy, scale=scale).then_inc(skip_ready, 1)

            def body(E, slot, beside):
                j = E - LATE
                act.wait_ge(delta_in[slot], (E - slot) * 8 + 16)
                for n in range(DS):
                    after(act, scan_done, E * DS + n - 1)
                    scale = a[:, bass.ds(E, 1), n:n + 1].rearrange("p o n -> p (o n)")
                    nc.scalar.activation(decay[:, n % 2, :], delta[:, slot, :], ACT.Exp, scale=scale).then_inc(decay_ready, 1)
                    if n == 1 and isinstance(E, int) and E == 0:
                        scale_skip(0)
                    if n == 12 and not (isinstance(E, int) and E == NBLK - 1):
                        scale_skip(E + 1)
                    if beside == 2:
                        if n == 1:
                            d.take_turned(act, j, 0, d.beside[slot])
                        if n == 3:
                            d.take_turned(act, j, 1, d.beside[slot])
                        if n == 5:
                            d.take_routing(act, j, d.beside[slot])
                        if n == 7:
                            d.exp_gap(act, j)
                            d.index_float(act, j)
                        if n == 8:
                            d.second_gate(act, j)
                        if n == 11:
                            d.take_gates(act, j, d.beside[slot])
                    if beside:
                        if n == 10:
                            d.row_sum(act, j + 1, 1 - slot)
                        if n == 11:
                            d.negative_mean(act, j + 1)
                        if n == 12:
                            d.squares(act, j + 1, 1 - slot)
                        if n == 13:
                            d.inverse_std(act, j + 1)
                        if n == 14:
                            d.norm_bias(act, j + 1)
                        if n == 15:
                            d.normalise(act, j + 1, 1 - slot)
            blocks(act, body)

            for i in range(2):
                d.take_turned(act, FIRST_TAIL, i, alone[0], True)

            def gates(j, at):
                d.take_routing(act, j, at)
                d.exp_gap(act, j)
                d.index_float(act, j)
                d.second_gate(act, j)
            gates(FIRST_TAIL, alone[0])

            def tail(j, slot, more=2):
                if more:
                    d.row_sum(act, j + 1, 1 - slot)
                    d.negative_mean(act, j + 1)
                    d.squares(act, j + 1, 1 - slot)
                    d.inverse_std(act, j + 1)
                    d.norm_bias(act, j + 1)
                d.take_gates(act, j, alone[slot])
                if more:
                    d.normalise(act, j + 1, 1 - slot)
                    d.take_turned(act, j + 1, 0, alone[1 - slot], True)
                    d.take_turned(act, j + 1, 1, alone[1 - slot], True)
                    gates(j + 1, alone[1 - slot])
            tail_tiles(act, tail)

        @block.vector
        def _(dve):
            d.set_constants(dve)

            def drive(E, slot, n):
                if n == 0:
                    dve.wait_ge(du_in[slot], (E - slot) * 8 + 16)
                dve.wait_ge(b_ready, E * DS + n + 1)
                nc.vector.tensor_tensor(row[n % 2][:, :], du[:, slot, :], row[n % 2][:, :], ALU.mult).then_inc(dbu_ready, 1)

            def scan(E, n):
                dve.wait_ge(dbu_ready, E * DS + n + 1)
                dve.wait_ge(decay_ready, E * DS + n + 1)
                after(dve, prod_ready, E * DS + n - 1)
                nc.vector.tensor_tensor_scan(state[:, n % 2, :], decay[:, n % 2, :], row[n % 2][:, :], 0.0,
                                             ALU.mult, ALU.add).then_inc(scan_done, 1)

            def gated_y(E):
                dve.wait_ge(summed, E * DS + DS)
                dve.wait_ge(gate_in, E * 16 + 16)
                after(dve, yy_out, E * 16)
                nc.vector.tensor_tensor(yy[:, :], gate[:, :], y_ps[:, :], ALU.mult).then_inc(yy_ready, 1)

            def body(E, slot, beside):
                j = E - LATE
                for n in range(DS):
                    drive(E, slot, n)
                    if n == 2 and not (isinstance(E, int) and E == 0):
                        gated_y(E - 1)
                    if beside == 2:
                        if n == 6:
                            d.largest(dve, j)
                        if n == 8:
                            d.first_gate(dve, j)
                        if n == 9:
                            d.gate_mask(dve, j, 0)
                        if n == 10:
                            d.gate_row(dve, j)
                        if n == 5 and not (isinstance(E, int) and E == LATE):
                            d.add_residual(dve, j - 1, 1 - slot, 1)
                        if n == 15:
                            d.add_residual(dve, j, slot, 0)
                    scan(E, n)
                    if beside == 2:
                        if n == 6:
                            d.chosen(dve, j)
                        if n == 9:
                            d.gate_mask(dve, j, 1)
                        if n == 10:
                            d.gated(dve, j)
            blocks(dve, body)
            d.add_residual(dve, FIRST_TAIL - 1, 1, 1)
            gated_y(NBLK - 1)

            def gates(j):
                d.largest(dve, j)
                d.chosen(dve, j)
                d.first_gate(dve, j)
                d.gate_mask(dve, j, 0)
                d.gate_mask(dve, j, 1)
                d.gate_row(dve, j)
                d.gated(dve, j)
            gates(FIRST_TAIL)

            def tail(j, slot, more=2):
                d.add_residual(dve, j, slot, 0)
                if more:
                    gates(j + 1)
                d.add_residual(dve, j, slot, 1)
            tail_tiles(dve, tail)

        @block.gpsimd
        def _(pool):
            def body(E, slot, beside, b):
                for n in range(DS):
                    if isinstance(E, int) and E % NE == 0:
                        pool.wait_ge(c_in[n], b * 16 + 16)
                    pool.wait_ge(scan_done, E * DS + n + 1)
                    after(pool, summed, E * DS + n - 1)
                    nc.gpsimd.tensor_tensor(prod[:, n % 2, :], state[:, n % 2, :], c_all[:, n, :], ALU.mult).then_inc(prod_ready, 1)
                    add_at = (6, 8) if isinstance(E, int) and E % NE == 0 else (4, 7)
                    if beside and n in add_at:
                        d.add_x(pool, E - LATE + 1, 1 - slot, add_at.index(n))
            blocks(pool, body, batch_ends)

            def tail(j, slot, more=2):
                if more:
                    d.add_x(pool, j + 1, 1 - slot, 0)
                    d.add_x(pool, j + 1, 1 - slot, 1)
            tail_tiles(pool, tail)


def program(nc, t, out):
    u_d, delta_d, du_d, gate_d, yy_d = (
        nc.dram_tensor(name, (B, DI, L), FP32, kind="Internal").ap() for name in ("u_d", "delta_d", "du_d", "gate_d", "yy_d"))
    parts_d = nc.dram_tensor("parts_d", (B, 96, L), BF16, kind="Internal").ap()
    c_d = nc.dram_tensor("c_d", (B, DS, L), FP32, kind="Internal").ap()
    front_stage(nc, t, u_d, delta_d, du_d, gate_d, parts_d, c_d)
    scan_stage(nc, t, u_d, delta_d, du_d, gate_d, parts_d, c_d, yy_d, out)


def kernel(**inputs):
    import numpy as np
    import concourse.bacc as bacc
    from concourse.bass_utils import run_bass_kernel_spmd as run

    i = {k: np.asarray(v) for k, v in inputs.items()}
    w_x = i["L0_xattn_x_proj_w"]
    bc = w_x[DR:]
    pick = np.zeros((96, DS, P), np.float32)
    for n in range(DS):
        pick[n::32, n, :] = 1.0

    def by_partition(columns):
        return columns.reshape(NE, P, -1).transpose(1, 0, 2)

    arrays = {
        "x": i["x"],
        "ctxT": i["ctx_1024"].transpose(0, 2, 1),
        "w_inT": i["L0_xattn_in_proj_w"].T,
        "w_xT": np.concatenate([bc, bc, bc, w_x[:DR]], 0).T,
        "w_dtT": i["L0_xattn_dt_proj_w"].T,
        "chan": by_partition(np.concatenate([i["L0_xattn_conv_w"], i["L0_xattn_conv_b"][:, None], i["L0_xattn_dt_proj_b"][:, None]], 1)),
        "a_log": np.tile(by_partition(np.concatenate([i["L0_xattn_A_log"], i["L0_xattn_D"][:, None]], 1)), (1, B, 1)),
        "w_oT": i["L0_ffn_W_base"].T,
        "w_raT": np.concatenate([i["L0_ffn_A_w"].reshape(NEX * RANK, DI), i["L0_ffn_W_router"]], 0).T,
        "w_bT": np.concatenate([i["L0_ffn_B_w"].transpose(0, 2, 1).reshape(NEX * RANK, DI), i["L0_ffn_b_base"][None]], 0),
        "pick": pick.astype(mybir.dt.np(BF16)),
        "ident": np.eye(P, dtype=np.float32),
        "iota": np.tile(np.arange(NEX, dtype=np.float32), (P, 1)),
    }
    nc = bacc.Bacc("TRN2", target_bir_lowering=False, num_devices=1)
    t = {}
    for name, a in arrays.items():
        arrays[name] = a = np.ascontiguousarray(a)
        t[name] = nc.dram_tensor(f"in_{name}", a.shape, mybir.dt.from_np(a.dtype), kind="ExternalInput").ap()
    out = nc.dram_tensor("out", (B, L, DI), FP32, kind="ExternalOutput").ap()
    program(nc, t, out)
    r = run(nc, [{f"in_{name}": a for name, a in arrays.items()}], core_ids=[0])
    return r.results[0]["out"]
```
